# Optimizing a Trainium2 kernel written in Bass

```python
import numpy as np
import jax
import jax.numpy as jnp

def _softmax(x, axis=-1):
    return jax.nn.softmax(x, axis=axis)

def _gelu(x):
    return jax.nn.gelu(x, approximate=True)

def _silu(x):
    return jax.nn.silu(x)

def _sigmoid(x):
    return jax.nn.sigmoid(x)

def _layernorm(x, axis=-1, eps=1e-05):
    m = jnp.mean(x, axis=axis, keepdims=True)
    v = jnp.var(x, axis=axis, keepdims=True)
    return (x - m) / jnp.sqrt(v + eps)

def _scatter_add(tgt, idx, src, axis=0):
    return tgt.at[idx].add(src)

def _segment_sum(src, seg, n):
    return jax.ops.segment_sum(src, seg, n)
kernel_name = 'mk_adaln_ffn_d2_seqx_r4_a27a66'

def setup_inputs(seed: int=0):
    np.random.seed(seed)
    _w = jnp.asarray

    def _rec_inputs():
        import jax
        import jax.numpy as jnp
        _rk = jax.random.key(seed)
        x = -0.000125 + 0.9999 * jax.random.normal(jax.random.fold_in(_rk, 1), (32, 64, 1024), jnp.float32)
        _lenS = 64 - jax.random.randint(jax.random.fold_in(_rk, 7), (32,), 0, max(1, 64 // 4) + 1, jnp.int32)
        _lenS2 = 64 - jax.random.randint(jax.random.fold_in(_rk, 8), (32,), 0, max(1, 64 // 4) + 1, jnp.int32)
        cond_128 = 0.0061147 + 1.02565 * jax.random.normal(jax.random.fold_in(_rk, 11), (32, 128), jnp.float32)
        fside_S_0 = -0.022604 + 0.987366 * jax.random.normal(jax.random.fold_in(_rk, 12), (64,), jnp.float32)
        return (x, cond_128, fside_S_0)
    x, cond_128, fside_S_0 = _rec_inputs()

    def _L0_cond_setup():
        import jax, jax.numpy as jnp
        import numpy as np
        from jax import lax
        N, C_IN, L = (32, 64, 1024)
        C_OUT, K, GROUPS = (64, 9, 4)
        C_DIM, PAD, STRIDE = (128, 4, 1)
        key = jax.random.key(seed)
        k1, k2, k3, k4, k5 = jax.random.split(key, 5)
        x = jax.random.normal(k1, (N, C_IN, L), dtype=jnp.float32)
        c = jax.random.normal(k2, (N, C_DIM), dtype=jnp.float32)
        weight = jax.random.normal(k3, (C_OUT, C_IN // GROUPS, K), dtype=jnp.float32)
        c_weight = jax.random.normal(k4, (C_OUT, C_DIM), dtype=jnp.float32)
        bias = jax.random.normal(k5, (C_OUT,), dtype=jnp.float32)
        return {'x': x, 'c': c, 'weight': weight, 'c_weight': c_weight, 'bias': bias}
    _L0_cond_all = _L0_cond_setup()
    _L0_cond_in = {k: v for k, v in _L0_cond_all.items() if k in ('weight', 'c_weight')}
    del _L0_cond_all

    def _L0_ffn_setup():
        import jax, jax.numpy as jnp
        import numpy as np
        NF4 = jnp.array([-1.0, -0.6961928009986877, -0.5250730514526367, -0.39491748809814453, -0.28444138169288635, -0.18477343022823334, -0.09105003625154495, 0.0, 0.07958029955625534, 0.16093020141124725, 0.24611230194568634, 0.33791524171829224, 0.44070982933044434, 0.5626170039176941, 0.7229568362236023, 1.0], dtype=jnp.float32)
        BLOCK = 64
        B, S, D, H, R = (2, 512, 1024, 2752, 16)

        def dequant_nf4(codes, absmax, shape):
            vals = NF4[codes] * jnp.repeat(absmax, BLOCK)
            return vals.reshape(shape)
        key = jax.random.key(seed)
        ks = jax.random.split(key, 11)
        n_w = H * D
        return {'x1': jax.random.normal(ks[0], (B, S, D), dtype=jnp.float32), 'w_up_codes': jax.random.randint(ks[1], (n_w,), 0, 16, dtype=jnp.int32), 'w_up_absmax': jax.random.uniform(ks[2], (n_w // BLOCK,), dtype=jnp.float32) * 0.05, 'b_up': jax.random.normal(ks[3], (H,), dtype=jnp.float32) * 0.02, 'w_up_lora_a': jax.random.normal(ks[4], (D, R), dtype=jnp.float32) * 0.02, 'w_up_lora_b': jax.random.normal(ks[5], (R, H), dtype=jnp.float32) * 0.02, 'w_down_codes': jax.random.randint(ks[6], (n_w,), 0, 16, dtype=jnp.int32), 'w_down_absmax': jax.random.uniform(ks[7], (n_w // BLOCK,), dtype=jnp.float32) * 0.05, 'b_down': jax.random.normal(ks[8], (D,), dtype=jnp.float32) * 0.02, 'w_down_lora_a': jax.random.normal(ks[9], (H, R), dtype=jnp.float32) * 0.02, 'w_down_lora_b': jax.random.normal(ks[10], (R, D), dtype=jnp.float32) * 0.02}
    _L0_ffn_all = _L0_ffn_setup()
    _L0_ffn_in = {k: v for k, v in _L0_ffn_all.items() if k in ('w_up_codes', 'w_up_absmax', 'b_up', 'w_up_lora_a', 'w_up_lora_b', 'w_down_codes', 'w_down_absmax', 'b_down', 'w_down_lora_a', 'w_down_lora_b')}
    del _L0_ffn_all

    def _L1_cond_setup():
        import jax, jax.numpy as jnp
        import numpy as np
        K = 8
        T = 1.0
        D_EMBD = 128
        IN_C = 64
        OUT_C = 64
        BS = 32
        H = 1024
        HID = 128
        key = jax.random.key(seed)
        ks = jax.random.split(key, 10)
        s = lambda fan_in: 1.0 / np.sqrt(fan_in)
        return {'x': jax.random.normal(ks[0], (BS, IN_C, H), dtype=jnp.float32), 'embedding': jax.random.normal(ks[1], (BS, D_EMBD), dtype=jnp.float32), 'W0': jax.random.normal(ks[2], (D_EMBD, HID), dtype=jnp.float32) * s(D_EMBD), 'b0': jnp.zeros((HID,), dtype=jnp.float32), 'W1': jax.random.normal(ks[3], (HID, HID), dtype=jnp.float32) * s(HID), 'b1': jnp.zeros((HID,), dtype=jnp.float32), 'W2': jax.random.normal(ks[4], (HID, K), dtype=jnp.float32) * s(HID), 'b2': jnp.zeros((K,), dtype=jnp.float32), 'weight': jax.random.normal(ks[5], (K, OUT_C, IN_C, 1), dtype=jnp.float32) * s(IN_C), 'bias_k': jax.random.normal(ks[6], (K, OUT_C), dtype=jnp.float32) * 0.1}
    _L1_cond_all = _L1_cond_setup()
    _L1_cond_in = {k: v for k, v in _L1_cond_all.items() if k in ('W0', 'b0', 'W1', 'b1', 'W2', 'b2', 'weight', 'bias_k')}
    del _L1_cond_all

    def _L1_ffn_setup():
        import jax, jax.numpy as jnp
        import numpy as np
        NUM_EXPERTS = 8
        D_IN = 1024
        D_OUT = 1024
        key = jax.random.key(seed)
        k_x, k_gw, k_gb, k_ew, k_eb = jax.random.split(key, 5)
        x = jax.random.normal(k_x, (4, 512, D_IN), dtype=jnp.float32)
        gate_w = jax.random.normal(k_gw, (NUM_EXPERTS, D_IN), dtype=jnp.float32) * 0.02
        gate_b = jax.random.normal(k_gb, (NUM_EXPERTS,), dtype=jnp.float32) * 0.02
        expert_w = jax.random.normal(k_ew, (NUM_EXPERTS, D_OUT, D_IN), dtype=jnp.float32) * 0.02
        expert_b = jax.random.normal(k_eb, (NUM_EXPERTS, D_OUT), dtype=jnp.float32) * 0.02
        return {'x': x, 'gate_w': gate_w, 'gate_b': gate_b, 'expert_w': expert_w, 'expert_b': expert_b}
    _L1_ffn_all = _L1_ffn_setup()
    _L1_ffn_in = {k: v for k, v in _L1_ffn_all.items() if k in ('gate_w', 'gate_b', 'expert_w', 'expert_b')}
    del _L1_ffn_all
    return {'x': x, 'cond_128': cond_128, 'fside_S_0': fside_S_0, 'L0_cond_weight': _L0_cond_in['weight'], 'L0_cond_c_weight': _L0_cond_in['c_weight'], 'L0_ffn_w_up_codes': _L0_ffn_in['w_up_codes'], 'L0_ffn_w_up_absmax': _L0_ffn_in['w_up_absmax'], 'L0_ffn_b_up': _L0_ffn_in['b_up'], 'L0_ffn_w_up_lora_a': _L0_ffn_in['w_up_lora_a'], 'L0_ffn_w_up_lora_b': _L0_ffn_in['w_up_lora_b'], 'L0_ffn_w_down_codes': _L0_ffn_in['w_down_codes'], 'L0_ffn_w_down_absmax': _L0_ffn_in['w_down_absmax'], 'L0_ffn_b_down': _L0_ffn_in['b_down'], 'L0_ffn_w_down_lora_a': _L0_ffn_in['w_down_lora_a'], 'L0_ffn_w_down_lora_b': _L0_ffn_in['w_down_lora_b'], 'L1_cond_W0': _L1_cond_in['W0'], 'L1_cond_b0': _L1_cond_in['b0'], 'L1_cond_W1': _L1_cond_in['W1'], 'L1_cond_b1': _L1_cond_in['b1'], 'L1_cond_W2': _L1_cond_in['W2'], 'L1_cond_b2': _L1_cond_in['b2'], 'L1_cond_weight': _L1_cond_in['weight'], 'L1_cond_bias_k': _L1_cond_in['bias_k'], 'L1_ffn_gate_w': _L1_ffn_in['gate_w'], 'L1_ffn_gate_b': _L1_ffn_in['gate_b'], 'L1_ffn_expert_w': _L1_ffn_in['expert_w'], 'L1_ffn_expert_b': _L1_ffn_in['expert_b']}

def reference(x, cond_128, fside_S_0, L0_cond_weight, L0_cond_c_weight, L0_ffn_w_up_codes, L0_ffn_w_up_absmax, L0_ffn_b_up, L0_ffn_w_up_lora_a, L0_ffn_w_up_lora_b, L0_ffn_w_down_codes, L0_ffn_w_down_absmax, L0_ffn_b_down, L0_ffn_w_down_lora_a, L0_ffn_w_down_lora_b, L1_cond_W0, L1_cond_b0, L1_cond_W1, L1_cond_b1, L1_cond_W2, L1_cond_b2, L1_cond_weight, L1_cond_bias_k, L1_ffn_gate_w, L1_ffn_gate_b, L1_ffn_expert_w, L1_ffn_expert_b):
    import jax
    import jax.numpy as jnp

    def _L0_cond_ref(x, c, weight, c_weight, bias):
        import jax, jax.numpy as jnp
        import numpy as np
        from jax import lax
        N, C_IN, L = (32, 64, 1024)
        C_OUT, K, GROUPS = (64, 9, 4)
        C_DIM, PAD, STRIDE = (128, 4, 1)
        out = lax.conv_general_dilated(x, weight, window_strides=(STRIDE,), padding=[(PAD, PAD)], dimension_numbers=('NCH', 'OIH', 'NCH'), feature_group_count=GROUPS)
        ctx = jnp.einsum('nd,od->no', c, c_weight)
        out = out + ctx[:, :, None] + bias[None, :, None]
        return out

    def _L0_ffn_ref(x1, w_up_codes, w_up_absmax, b_up, w_up_lora_a, w_up_lora_b, w_down_codes, w_down_absmax, b_down, w_down_lora_a, w_down_lora_b):
        import jax, jax.numpy as jnp
        import numpy as np
        NF4 = jnp.array([-1.0, -0.6961928009986877, -0.5250730514526367, -0.39491748809814453, -0.28444138169288635, -0.18477343022823334, -0.09105003625154495, 0.0, 0.07958029955625534, 0.16093020141124725, 0.24611230194568634, 0.33791524171829224, 0.44070982933044434, 0.5626170039176941, 0.7229568362236023, 1.0], dtype=jnp.float32)
        BLOCK = 64
        B, S, D, H, R = (2, 512, 1024, 2752, 16)

        def dequant_nf4(codes, absmax, shape):
            vals = NF4[codes] * jnp.repeat(absmax, BLOCK)
            return vals.reshape(shape)
        w_up = dequant_nf4(w_up_codes, w_up_absmax, (H, D)).T
        y1 = x1 @ w_up + b_up + x1 @ w_up_lora_a @ w_up_lora_b
        x2 = jax.nn.relu(y1)
        w_down = dequant_nf4(w_down_codes, w_down_absmax, (D, H)).T
        y2 = x2 @ w_down + b_down + x2 @ w_down_lora_a @ w_down_lora_b
        return y2

    def _L1_cond_ref(x, embedding, W0, b0, W1, b1, W2, b2, weight, bias_k):
        import jax, jax.numpy as jnp
        import numpy as np
        K = 8
        T = 1.0
        D_EMBD = 128
        IN_C = 64
        OUT_C = 64
        BS = 32
        H = 1024
        HID = 128
        h = jax.nn.gelu(embedding @ W0 + b0, approximate=False)
        h = jax.nn.gelu(h @ W1 + b1, approximate=False)
        att = jax.nn.softmax((h @ W2 + b2) / T, axis=-1)
        agg_w = jnp.einsum('bk,koi->boi', att, weight[..., 0])
        agg_b = att @ bias_k
        out = jnp.einsum('boi,bih->boh', agg_w, x) + agg_b[:, :, None]
        return out

    def _L1_ffn_ref(x, gate_w, gate_b, expert_w, expert_b):
        import jax, jax.numpy as jnp
        import numpy as np
        NUM_EXPERTS = 8
        D_IN = 1024
        D_OUT = 1024
        orig_shape = x.shape
        xf = x.reshape(-1, x.shape[-1])
        gate_logits = xf @ gate_w.T + gate_b
        gates = jax.nn.softmax(gate_logits, axis=-1)
        selected = jnp.argmax(gates, axis=-1)
        out = jnp.zeros((xf.shape[0], expert_w.shape[1]), dtype=xf.dtype)
        for j in range(expert_w.shape[0]):
            yj = xf @ expert_w[j].T + expert_b[j]
            out = out + jnp.where((selected == j)[:, None], yj, 0.0)
        return out.reshape(*orig_shape[:-1], expert_w.shape[1])
    x = x + _L0_ffn_ref(_L0_cond_ref(x, cond_128, L0_cond_weight, L0_cond_c_weight, fside_S_0), L0_ffn_w_up_codes, L0_ffn_w_up_absmax, L0_ffn_b_up, L0_ffn_w_up_lora_a, L0_ffn_w_up_lora_b, L0_ffn_w_down_codes, L0_ffn_w_down_absmax, L0_ffn_b_down, L0_ffn_w_down_lora_a, L0_ffn_w_down_lora_b)
    x = x + _L1_ffn_ref(_L1_cond_ref(x, cond_128, L1_cond_W0, L1_cond_b0, L1_cond_W1, L1_cond_b1, L1_cond_W2, L1_cond_b2, L1_cond_weight, L1_cond_bias_k), L1_ffn_gate_w, L1_ffn_gate_b, L1_ffn_expert_w, L1_ffn_expert_b)
    return x

_drawn_inputs = setup_inputs


def setup_inputs(seed=0):
    import zlib

    import numpy as np

    out = dict(_drawn_inputs(seed))
    spreads = {'L1_cond_b0': (0.0, 0.1), 'L1_cond_b1': (0.0, 0.1), 'L1_cond_b2': (0.0, 0.1)}
    factors = {'L0_ffn_b_up': 18.284,
     'L0_ffn_b_down': 6.886,
     'L1_cond_bias_k': 6.573,
     'L1_ffn_gate_b': 3.125,
     'L1_ffn_expert_b': 30.547}
    for name, (base, spread) in spreads.items():
        noise = np.random.default_rng([zlib.crc32(name.encode()), seed]).standard_normal(out[name].shape)
        drawn = base * np.exp(spread * noise) if base else spread * noise
        out[name] = jnp.asarray(drawn.astype(out[name].dtype))
    for name, factor in factors.items():
        out[name] = (out[name] * factor).astype(out[name].dtype)
    return out
```

```python
from contextlib import ExitStack

import concourse.bass as bass
import numpy as np
from concourse import mybir

F32 = mybir.dt.float32
F32R = mybir.dt.float32r
I32 = mybir.dt.int32
U32 = mybir.dt.uint32
ALU = mybir.AluOpType
ACT = mybir.ActivationFunctionType
AX = mybir.AxisListType

P = 128
B, CH, L = 32, 64, 1024
GROUPS, TAPS = 4, 9
GC = CH // GROUPS
J = P // GC
MB = L // J + 1
N = B * CH
BLKS = 2
NB = N // BLKS
BB = B // BLKS
HID = 2752
NT = -(-HID // P)
NG = NT // 2
HALF = 512
NU = 2 * NG
JOBS = 4 * NG
KT = L // P
R = 16
E = 8
PAIRS = BB // 2
TILES = N // P
ST = 256
NS = (N + E * (ST - 1)) // ST
SC = NS * ST // P
ONEHOT = 4

NF4 = np.array([-1.0, -0.6961928009986877, -0.5250730514526367, -0.39491748809814453, -0.28444138169288635,
                -0.18477343022823334, -0.09105003625154495, 0.0, 0.07958029955625534, 0.16093020141124725,
                0.24611230194568634, 0.33791524171829224, 0.44070982933044434, 0.5626170039176941,
                0.7229568362236023, 1.0], np.float32)


def nf4_terms():
    f, terms = NF4.astype(np.float64), []
    for sign, near in ((1, 8), (-1, 7)):
        slope = base = 0.0
        side = []
        for n in range(4):
            c = near + 2 * sign * n
            new_slope = sign * (f[c + sign] - f[c])
            new_base = f[c] - new_slope * c
            side.append((float(sign), float((base - new_base) / (new_slope - slope)), float(sign * (new_slope - slope))))
            slope, base = new_slope, new_base
        terms += side[::-1]
    return terms


def wait(eng, sem, value):
    if isinstance(value, int) and value <= 0:
        return
    eng.wait_ge(sem, value)


def rounds(eng, n):
    yield 0
    with eng.Fori(1, n) as i:
        yield i


def program(nc, x_nat, x_conv, toep, cond_t, ctx_w_t, chan_bias, codes_up, codes_dn, am_up, am_dn, bias_up, bias_dn,
            lora_up_at, lora_up_b, lora_dn_at, lora_dn_b, w0, b0, w1, b1, w2, b2, kern, kern_b, gate_t, gate_b,
            exp_w, exp_b, out):
    TERMS = nf4_terms()
    NTM = len(TERMS)
    STT = NTM - 1
    ctx = ExitStack()
    with ctx:
        def sem(name):
            return ctx.enter_context(nc.semaphore(name))

        def sb(stack, name, shape, dt=F32):
            return stack.enter_context(nc.sbuf_tensor(name, shape, dt))

        w_dram = nc.dram_tensor("w_dequantised", (JOBS, P, L), F32, kind="Internal").ap()
        zx_dram = nc.dram_tensor("z_and_x_rows", (N, 2 * L), F32, kind="Internal").ap()
        slot_dram = nc.dram_tensor("slot_token", (P * SC, 1), I32, kind="Internal").ap()

        ident = sb(ctx, "ident", [P, P])
        ones = sb(ctx, "ones", [P, P])
        att_t = sb(ctx, "att_t", [E, B])
        logits = sb(ctx, "logits", [P, TILES, E])

        late = ExitStack()
        acc = sb(late, "acc", [P, PAIRS, L])
        x1h = sb(late, "x1h", [P, KT, NB], F32R)
        x1l = sb(late, "x1l", [P, KT, NB], F32R)
        v = sb(late, "v", [P, 2, L])

        ffn = ExitStack()
        wuh = sb(ffn, "wuh", [P, 4, L], F32R)
        wul = sb(ffn, "wul", [P, 4, L], F32R)
        wdh = sb(ffn, "wdh", [P, 4, L], F32R)
        wdl = sb(ffn, "wdl", [P, 4, L], F32R)
        hh = sb(ffn, "hh", [P, 4, HALF], F32R)
        hl = sb(ffn, "hl", [P, 4, HALF], F32R)
        term = sb(ffn, "term", [P, 2, 512])
        codes = sb(ffn, "codes", [P, 2, L], I32)
        amu = sb(ffn, "amu", [P, 2, P])
        amd = sb(ffn, "amd", [P, L])
        lora = sb(ffn, "lora", [48, L])
        lora_t = sb(ffn, "lora_t", [48, 2, P])
        bup = sb(ffn, "bup", [P, NT])
        ffn.close()

        conv = ExitStack()
        xcv = sb(conv, "xcv", [P, 2, 2, GROUPS, MB])
        tz = sb(conv, "tz", [P, 2, GROUPS, P])
        ct = sb(conv, "ct", [P, B])
        cwt = sb(conv, "cwt", [P, CH])
        cbias = sb(conv, "cbias", [1, CH])
        cprod = sb(conv, "cprod", [P, BB, CH])
        ctxb = sb(conv, "ctxb", [P, NB])
        x32 = sb(conv, "x32", [P, 2, KT, CH])
        conv.close()

        dyn = ExitStack()
        ct2 = sb(dyn, "ct2", [P, B])
        w0s = sb(dyn, "w0s", [P, P])
        w1s = sb(dyn, "w1s", [P, P])
        w2s = sb(dyn, "w2s", [P, E])
        b0s = sb(dyn, "b0s", [P, 1])
        b1s = sb(dyn, "b1s", [P, 1])
        b2s = sb(dyn, "b2s", [1, E])
        hid1 = sb(dyn, "hid1", [P, B])
        hid2 = sb(dyn, "hid2", [P, B])
        satt = sb(dyn, "satt", [B, 3 * E])
        kerns = sb(dyn, "kerns", [E, CH, P])
        kernb = sb(dyn, "kernb", [E, P])
        gts = sb(dyn, "gts", [P, KT, E])
        gbs = sb(dyn, "gbs", [1, E])
        agg = sb(dyn, "agg", [P, CH, BB])
        aggb = sb(dyn, "aggb", [P, PAIRS])
        bdg = sb(dyn, "bdg", [P, 2, P])
        z32 = sb(dyn, "z32", [P, 2, L])
        zt = sb(dyn, "zt", [P, 2, L])
        dyn.close()
        late.close()

        moe = ExitStack()
        whr = sb(moe, "whr", [P, 4, L], F32R)
        wlr = sb(moe, "wlr", [P, 4, L], F32R)
        zth = sb(moe, "zth", [P, 2, KT, ST], F32R)
        ztl = sb(moe, "ztl", [P, 2, KT, ST], F32R)
        wraw = sb(moe, "wraw", [P, KT, L])
        zx = sb(moe, "zx", [P, 2, 2, 2 * L])
        ebs = sb(moe, "ebs", [P, 2, L])
        tri = sb(moe, "tri", [P, P])
        top = sb(moe, "top", [P, TILES, E])
        topi = sb(moe, "topi", [P, TILES, E], U32)
        eid = sb(moe, "eid", [P, TILES])
        iota_e = sb(moe, "iota_e", [P, E], I32)
        iota_ef = sb(moe, "iota_ef", [P, E])
        iota_s = sb(moe, "iota_s", [P, 16], I32)
        iota_sf = sb(moe, "iota_sf", [P, 16])
        oh = sb(moe, "oh", [P, TILES, E])
        run = sb(moe, "run", [P, TILES + 1, E])
        cnt = sb(moe, "cnt", [P, E], I32)
        cnt2 = sb(moe, "cnt2", [P, E], I32)
        ntl = sb(moe, "ntl", [P, E])
        end = sb(moe, "end", [P, E + 1])
        place = sb(moe, "place", [P, TILES, E])
        slotf = sb(moe, "slotf", [P, TILES])
        sloti = sb(moe, "sloti", [P, 4, TILES], I32)
        slotp = sb(moe, "slotp", [P, 2, TILES])
        tokid = sb(moe, "tokid", [P, TILES], I32)
        nobody = sb(moe, "nobody", [P, SC], I32)
        table = sb(moe, "table", [P, SC], I32)
        past = sb(moe, "past", [P, 16, E])
        etf = sb(moe, "etf", [P, 16])
        eti = sb(moe, "eti", [P, 16], I32)
        ridx = sb(moe, "ridx", [P, 4], I32)
        moe.close()

        bank = [ctx.enter_context(nc.psum_tensor(f"bank{i}", [P, 512], F32)) for i in range(8)]

        ident_ready, ones_ready = sem("ident_ready"), sem("ones_ready")
        conv_const = sem("conv_const")
        xcv_in = [sem(f"xcv_in{i}") for i in range(2)]
        acc_in, bdn_in = sem("acc_in"), sem("bdn_in")
        cprod_ready, ctx_mm, ctxb_ready = sem("cprod_ready"), sem("ctx_mm"), sem("ctxb_ready")
        conv_mm, x32_ready, x1h_ready, x1l_ready = sem("conv_mm"), sem("x32_ready"), sem("x1h_ready"), sem("x1l_ready")
        acc_bias = sem("acc_bias")
        ffn_const = sem("ffn_const")
        codes_in = [sem(f"codes_in{i}") for i in range(2)]
        amu_in, amd_in = [sem(f"amu_in{i}") for i in range(2)], sem("amd_in")
        lora_in = [sem(f"lora_in{i}") for i in range(2)]
        term_ready, term_added, scaled, ab_mm, w_ready = (sem(n) for n in (
            "term_ready", "term_added", "scaled", "ab_mm", "w_ready"))
        w_stored = [sem(f"w_stored{i}") for i in range(2)]
        w_in = [sem(f"w_in{i}") for i in range(2)]
        wh_ready, wl_ready = sem("wh_ready"), sem("wl_ready")
        up_mm, relu_done, hh_ready, hl_ready = sem("up_mm"), sem("relu_done"), sem("hh_ready"), sem("hl_ready")
        dn_mm, acc_added = sem("dn_mm"), sem("acc_added")
        dyn_const, mlp_mm, mlp_act, mlp_dve, att_ready = (sem(n) for n in (
            "dyn_const", "mlp_mm", "mlp_act", "mlp_dve", "att_ready"))
        agg_mm, agg_ready, bdg_zero, bdg_ready = sem("agg_mm"), sem("agg_ready"), sem("bdg_zero"), sem("bdg_ready")
        z_mm, z_ready, z_tr, zt_ready, gate_mm, logit_ready = (sem(n) for n in (
            "z_mm", "z_ready", "z_tr", "zt_ready", "gate_mm", "logit_ready"))
        z_stored = [sem(f"z_stored{i}") for i in range(2)]
        x_stored = sem("x_stored")
        iotas, nobody_ready, table_clear, table_set, table_in = (sem(n) for n in (
            "iotas", "nobody_ready", "table_clear", "table_set", "table_in"))
        route_dve, route_mm, slots_ready, tiles_ready = (sem(n) for n in (
            "route_dve", "route_mm", "slots_ready", "tiles_ready"))
        zx_zero, ridx_ready = sem("zx_zero"), sem("ridx_ready")
        zx_in = [sem(f"zx_in{i}") for i in range(2)]
        wraw_in = [sem(f"wraw_in{i}") for i in range(KT)]
        eb_in = [sem(f"eb_in{i}") for i in range(2)]
        whr_ready, wlr_ready, chunk_mm = sem("whr_ready"), sem("wlr_ready"), sem("chunk_mm")
        tr_mm, zth_ready, ztl_ready = sem("tr_mm"), sem("zth_ready"), sem("ztl_ready")
        xb_ready, y_ready = sem("xb_ready"), sem("y_ready")
        out_done = [sem(f"out_done{i}") for i in range(2)]

        act_passed, pool_passed = sem("act_passed"), sem("pool_passed")

        block = ctx.enter_context(nc.Block())

        CONSTS_DYN = 11

        @block.sync
        def _(sp):
            for blk in range(BLKS):
                wait(sp, logit_ready, PAIRS * blk)
                for k in range(2):
                    wait(sp, z_stored[k], 16 * PAIRS // 2 * blk)
                for dst, src in ((tz[:], toep), (ct[:], cond_t), (cwt[:], ctx_w_t), (cbias[:], chan_bias)):
                    sp.dma_start(dst, src).then_inc(conv_const, 16)
                for i in rounds(sp, PAIRS // 2):
                    for k in range(2):
                        wait(sp, conv_mm, i * 4 + (BB * blk + 2 * k - 2) if not isinstance(i, int) or i else 0)
                        sp.dma_start(xcv[:, k], x_conv[:, bass.ds(i * 4 + (BB * blk + 2 * k), 2)]).then_inc(xcv_in[k], 16)
                wait(sp, x_stored, 16 * blk)
                sp.dma_start(acc[:], x_nat[blk * NB:(blk + 1) * NB].rearrange("(t p) l -> p t l", p=P)).then_inc(acc_in, 16)
                if blk:
                    for k in range(2):
                        wait(sp, w_stored[k], 16 * JOBS // 2)
                    wait(sp, wl_ready, JOBS)
                sp.dma_start(v[:, 0], bias_dn[0:1, :].broadcast_to([P, L])).then_inc(bdn_in, 16)
                wait(sp, x1l_ready, BB * (blk + 1))
                sp.dma_start(lora[0:R], lora_up_at).then_inc(ffn_const, 16)
                sp.dma_start(lora[32:32 + R], lora_dn_b).then_inc(ffn_const, 16)
                sp.dma_start(bup[:], bias_up).then_inc(ffn_const, 16)

                def load(g2, par, jj):
                    s = jj % 2
                    if blk == 0:
                        wait(sp, term_ready, g2 * (16 * NTM) + 2 * NTM * (4 * par + jj - 1))
                        t = g2 * 4 + (2 * par + s)
                        if jj < 2:
                            sp.dma_start(codes[:, s], codes_up[bass.ds(t, 1)].rearrange("a p n -> p (a n)")).then_inc(codes_in[s], 16)
                            wait(sp, scaled, g2 * 16 + 2 * (4 * par - 4 + s + 1))
                            sp.dma_start(amu[:, s], am_up[bass.ds(t, 1)].rearrange("a k (o n) -> (a k) o n", o=1)
                                         .broadcast_to([16, 8, P])).then_inc(amu_in[s], 16)
                            wait(sp, ab_mm, g2 * 8 + (4 * par - 4 + s + 3))
                            sp.dma_start(lora_t[0:R, s], lora_up_b[bass.ds(t, 1)].rearrange("a r n -> (a r) n")).then_inc(lora_in[s], 16)
                            sp.dma_start(lora_t[32:32 + R, s], lora_dn_at[bass.ds(t, 1)].rearrange("a r n -> (a r) n")).then_inc(lora_in[s], 16)
                        else:
                            sp.dma_start(codes[:, s], codes_dn[bass.ds(t, 1)].rearrange("a p n -> p (a n)")).then_inc(codes_in[s], 16)
                            wait(sp, scaled, g2 * 16 + 2 * (4 * par + (3 if jj == 3 else 0)))
                            sp.dma_start(amd[:], am_dn[bass.ds(t, 1)].rearrange("a k (o n) -> (a k) o n", o=1)
                                         .broadcast_to([2, 64, L])).then_inc(amd_in, 16)
                    else:
                        wait(sp, wl_ready, g2 * 8 + (JOBS + 4 * par + jj - 1))
                        sp.dma_start(v[:, s], w_dram[bass.ds(g2 * 8 + (4 * par + jj), 1)].rearrange("a p n -> p (a n)")).then_inc(w_in[s], 16)

                wait(sp, acc_bias, PAIRS * (blk + 1))
                for jj in range(4):
                    load(0, 0, jj)
                for i in rounds(sp, NG // 2):
                    for k in range(4):
                        for jj in (0, 1) if k % 2 == 0 else (2, 3):
                            load(i if k < 2 else i + 1, 1 if k < 2 else 0, jj)

                wait(sp, dn_mm, 8 * NU * (blk + 1))
                wait(sp, acc_added, 8 * NU * (blk + 1))
                if blk == 0:
                    for dst, src in ((ct2[:], cond_t), (w0s[:], w0), (w1s[:], w1), (w2s[:], w2), (b0s[:], b0), (b1s[:], b1),
                                     (b2s[:], b2)):
                        sp.dma_start(dst, src).then_inc(dyn_const, 16)
                for dst, src in ((kerns[:], kern), (kernb[:], kern_b), (gts[:], gate_t), (gbs[:], gate_b)):
                    sp.dma_start(dst, src).then_inc(dyn_const, 16)

            wait(sp, logit_ready, TILES)
            for k in range(2):
                wait(sp, z_stored[k], 16 * TILES // 2)
            wait(sp, x_stored, 32)
            wait(sp, nobody_ready, 1)
            sp.dma_start(slot_dram.rearrange("(p c) o -> p (c o)", p=P), nobody[:]).then_inc(table_clear, 16)
            wait(sp, table_set, 16 * TILES)
            sp.dma_start(table[:], slot_dram.rearrange("(p c) o -> p (c o)", p=P)).then_inc(table_in, 16)
            wait(sp, tiles_ready, 1)

            def load_expert(i, par):
                e = sp.value_load(eti[0:1, bass.ds(i * 2 + par, 1)], min_val=0, max_val=E - 1)
                for kt in range(KT):
                    wait(sp, wlr_ready, i * 16 + (8 * par + kt - 7))
                    sp.dma_start(wraw[:, kt], exp_w[bass.ds(e, 1), :, kt].rearrange("a p n -> p (a n)")).then_inc(wraw_in[kt], 16)
                wait(sp, xb_ready, i * 2 + (par - 1))
                sp.dma_start(ebs[:, par], exp_b[bass.ds(e, 1)].broadcast_to([P, L])).then_inc(eb_in[par], 16)

            for i in rounds(sp, NS // 2):
                load_expert(i, 0)
                load_expert(i, 1)
            load_expert(NS // 2, 0)

        @block.gpsimd
        def _(pool):
            last_row = pool.to_reg(N - 1)
            nc.gpsimd.memset(ident[:], 0.0).then_inc(ident_ready, 1)
            nc.gpsimd.memset(ones[:], 1.0).then_inc(ones_ready, 1)
            pool.wait_ge(ident_ready, 1)
            nc.gpsimd.affine_select(out=ident[:], in_=ident[:], compare_op=ALU.not_equal, fill=1.0, base=0,
                                    pattern=[[-1, P]], channel_multiplier=1).then_inc(ident_ready, 1)

            def store(i, par, jj):
                wait(pool, w_ready, i * 16 + 2 * (4 * par + jj + 1))
                pool.dma_start(w_dram[bass.ds(i * 8 + (4 * par + jj), 1)].rearrange("a p n -> p (a n)"),
                               v[:, jj % 2]).then_inc(w_stored[jj % 2], 16)

            for blk in range(BLKS):
                if blk == 0:
                    for jj in range(4):
                        store(0, 0, jj)
                    for i in rounds(pool, NG // 2):
                        for k in range(4):
                            for jj in (0, 1) if k % 2 == 0 else (2, 3):
                                store(i if k < 2 else i + 1, 1 if k < 2 else 0, jj)
                wait(pool, acc_added, 8 * NU * (blk + 1))
                pool.dma_start(zx_dram[blk * NB:(blk + 1) * NB, L:].rearrange("(t p) l -> p t l", p=P), acc[:]).then_inc(x_stored, 16)
                for i in rounds(pool, PAIRS // 2):
                    for k in range(2):
                        wait(pool, z_ready, i * 4 + (2 * PAIRS * blk + 2 * k + 2))
                        pool.dma_start(zx_dram[bass.ds(i * 2 * P + (blk * NB + k * P), P), 0:L], z32[:, k]).then_inc(z_stored[k], 16)

            wait(pool, logit_ready, TILES)
            for k in range(2):
                wait(pool, z_stored[k], 16 * TILES // 2)
            wait(pool, x_stored, 32)
            nc.gpsimd.iota(iota_e[:], [[1, E]], base=0, channel_multiplier=0).then_inc(iotas, 1)
            nc.gpsimd.iota(iota_s[:], [[1, 16]], base=0, channel_multiplier=0).then_inc(iotas, 1)
            nc.gpsimd.iota(tokid[:], [[P, TILES]], base=0, channel_multiplier=1).then_inc(iotas, 1)
            nc.gpsimd.iota(nobody[:], [[0, SC]], base=1 << 20, channel_multiplier=0).then_inc(nobody_ready, 1)
            nc.gpsimd.memset(tri[:], 1.0).then_inc(iotas, 1)
            pool.wait_ge(iotas, 4)
            nc.gpsimd.affine_select(out=tri[:], in_=tri[:], compare_op=ALU.is_gt, fill=0.0, base=0,
                                    pattern=[[1, P]], channel_multiplier=-1).then_inc(iotas, 1)
            nc.gpsimd.memset(zx[:], 0.0).then_inc(zx_zero, 1)
            pool.wait_ge(slots_ready, 1)
            pool.wait_ge(table_clear, 16)
            for t in range(TILES):
                pool.indirect_dma_start(slot_dram, bass.IndirectOffsetOnAxis(sloti[:, 3, t:t + 1], 0),
                                        tokid[:, t:t + 1], None).then_inc(table_set, 16)
            pool.wait_ge(table_in, 16)
            pool.wait_ge(zx_zero, 1)

            def gather(i, par):
                wait(pool, out_done[par], i * 32)
                nc.gpsimd.tensor_copy(ridx[:, 2 * par:2 * par + 2], table[:, bass.ds(i * 4 + 2 * par, 2)]).then_inc(ridx_ready, 1)
                wait(pool, ridx_ready, i * 2 + (par + 1))
                pool.sem_inc(pool_passed, 1)
                for h in range(2):
                    pool.indirect_dma_start(zx[:, par, h], None, zx_dram,
                                            bass.IndirectOffsetOnAxis(ridx[:, 2 * par + h:2 * par + h + 1], 0),
                                            bounds_check=last_row, oob_is_err=False).then_inc(zx_in[par], 16)

            def scatter(i, par):
                wait(pool, y_ready, i * 8 + (4 * par + 4))
                pool.sem_inc(pool_passed, 1)
                for h in range(2):
                    pool.indirect_dma_start(out, bass.IndirectOffsetOnAxis(ridx[:, 2 * par + h:2 * par + h + 1], 0),
                                            zx[:, par, h, L:2 * L], None,
                                            bounds_check=last_row, oob_is_err=False).then_inc(out_done[par], 16)

            gather(0, 0)
            for i in rounds(pool, NS // 2):
                gather(i, 1)
                scatter(i, 0)
                gather(i + 1, 0)
                scatter(i, 1)
            scatter(NS // 2, 0)
            pool.wait_ge(out_done[0], 32 * (NS // 2 + 1))
            pool.wait_ge(out_done[1], 32 * (NS // 2))
            pool.wait_ge(w_stored[0], 16 * JOBS // 2)
            pool.wait_ge(w_stored[1], 16 * JOBS // 2)

        @block.scalar
        def _(act):
            for blk in range(BLKS):
                for i in rounds(act, BB // 4):
                    for k in range(4):
                        act.wait_ge(x32_ready, i * 4 + (BB * blk + k + 1))
                        act.sem_inc(act_passed, 1)
                        nc.scalar.activation(x1h[:, :, bass.ds(i * 4 * CH + k * CH, CH)], x32[:, k % 2], ACT.Copy).then_inc(x1h_ready, 1)

                def lookup(i, par, jj):
                    s, n = jj % 2, 4 * par + jj
                    act.wait_ge(codes_in[s], i * 64 + (16 * (n // 2) + 16))
                    for h in range(2):
                        for m, (sign, bend, _) in enumerate(TERMS):
                            taken = m - 1 if m < 2 else max(m - 2, 1)
                            wait(act, term_added, i * (16 * STT) + (STT * (2 * n + h) + taken))
                            nc.scalar.activation(term[:, m % 2], codes[:, s, h * 512:(h + 1) * 512], ACT.Relu, scale=sign,
                                                 bias=-sign * bend).then_inc(term_ready, 1)

                def high(i, par, jj):
                    s, n = jj % 2, 4 * par + jj
                    if blk == 0:
                        act.wait_ge(w_ready, i * 16 + 2 * (n + 1))
                    else:
                        act.wait_ge(w_in[s], i * 64 + (16 * (n // 2) + 16))
                    before = 2 * par - 2 + NU * blk
                    if jj < 2:
                        wait(act, up_mm, i * 4 + before)
                    else:
                        wait(act, dn_mm, i * 32 + 8 * before)
                    dst = wuh if jj < 2 else wdh
                    nc.scalar.activation(dst[:, 2 * par + s], v[:, s], ACT.Copy).then_inc(wh_ready, 1)

                def relu(i, w):
                    par = w % 2
                    act.wait_ge(up_mm, i * 4 + (NU * blk + w + 1))
                    act.sem_inc(act_passed, 1)
                    for s in range(2):
                        nc.scalar.activation(bank[s][:], bank[s][:], ACT.Relu,
                                             bias=bup[:, bass.ds(i * 4 + (2 * (w // 2) + s), 1)]).then_inc(relu_done, 1)
                    wait(act, dn_mm, i * 32 + 8 * (NU * blk + w - 1))
                    for s in range(2):
                        act.wait_ge(relu_done, i * 8 + (2 * (NU * blk + w) + s + 1))
                        nc.scalar.activation(hh[:, 2 * par + s], bank[s][:], ACT.Copy).then_inc(hh_ready, 1)

                act.wait_ge(ffn_const, 48 * (blk + 1))
                for jj in range(4):
                    if blk == 0:
                        lookup(0, 0, jj)
                    high(0, 0, jj)
                relu(0, 0)
                for i in rounds(act, NG // 2):
                    for k in range(4):
                        step = (i, 1) if k < 2 else (i + 1, 0)
                        a, b = (0, 1) if k % 2 == 0 else (2, 3)
                        if blk == 0:
                            lookup(*step, a)
                        high(*step, a)
                        relu(i, k + 1)
                        if blk == 0:
                            lookup(*step, b)
                        high(*step, b)
                relu(NG // 2, 1)

                if blk == 0:
                    act.wait_ge(dyn_const, 16 * 11)
                    act.wait_ge(mlp_mm, 1)
                    nc.scalar.activation(hid1[:], bank[0][:, 0:B], ACT.Gelu, bias=b0s[:, 0:1]).then_inc(mlp_act, 1)
                    act.wait_ge(mlp_mm, 2)
                    nc.scalar.activation(hid2[:], bank[1][:, 0:B], ACT.Gelu, bias=b1s[:, 0:1]).then_inc(mlp_act, 1)
                    act.wait_ge(mlp_dve, 2)
                    nc.scalar.activation(satt[:, 0:E], bank[2][0:B, 0:E], ACT.Exp, bias=satt[:, 2 * E:2 * E + 1],
                                         accum_out=satt[:, 2 * E + 1:2 * E + 2]).then_inc(mlp_act, 1)
                act.wait_ge(agg_ready, 4 * (blk + 1))
                for i in rounds(act, PAIRS // 2):
                    for k in range(2):
                        act.wait_ge(z_mm, i * 2 + (PAIRS * blk + k + 1))
                        wait(act, z_stored[k], i * 16 + (16 * PAIRS // 2 * blk))
                        wait(act, z_tr, i * 2 + (PAIRS * blk + k - 1))
                        for h in range(2):
                            nc.scalar.activation(z32[:, k, h * 512:(h + 1) * 512], bank[2 * k + h][:], ACT.Identity,
                                                 bias=aggb[:, bass.ds(i * 2 + k, 1)]).then_inc(z_ready, 1)

            def chunk_high(i, par, kt):
                act.wait_ge(wraw_in[kt], i * 32 + (16 * par + 16))
                wait(act, chunk_mm, i * 16 + (8 * par + kt - 3))
                nc.scalar.activation(whr[:, kt % 4], wraw[:, kt], ACT.Copy).then_inc(whr_ready, 1)

            def z_high(i, par):
                for b in range(4):
                    act.wait_ge(tr_mm, i * 8 + (4 * par + b + 1))
                    wait(act, chunk_mm, i * 16 + (8 * par - 8))
                    nc.scalar.activation(zth[:, par, 2 * b:2 * b + 2], bank[4 * par + b][:].rearrange("p (k s) -> p k s", k=2),
                                         ACT.Copy).then_inc(zth_ready, 1)

            def expert(i, par, nxt):
                for kt in range(KT):
                    chunk_high(i, par, kt)
                    if kt == 5 and nxt:
                        z_high(*nxt)

            wait(act, logit_ready, TILES)
            for k in range(2):
                wait(act, z_stored[k], 16 * TILES // 2)
            z_high(0, 0)
            for i in rounds(act, NS // 2):
                expert(i, 0, (i, 1))
                expert(i, 1, (i + 1, 0))
            expert(NS // 2, 0, None)

        @block.vector
        def _(dve):
            for blk in range(BLKS):
                dve.wait_ge(conv_const, 64 * (blk + 1))
                cb = ct[:, BB * blk:BB * (blk + 1)].rearrange("p (b o) -> p b o", o=1).broadcast_to([P, BB, CH])
                cw = cwt[:].rearrange("p (b o) -> p b o", b=1).broadcast_to([P, BB, CH])
                nc.vector.tensor_tensor(cprod[:], cb, cw, ALU.mult).then_inc(cprod_ready, 1)
                dve.wait_ge(ctx_mm, blk + 1)
                for h in range(2):
                    nc.vector.tensor_copy(ctxb[:, h * 512:(h + 1) * 512], bank[h][:]).then_inc(ctxb_ready, 1)
                dve.wait_ge(ctxb_ready, 2 * (blk + 1))

                def conv_low(i, k):
                    dve.wait_ge(x1h_ready, i * 4 + (BB * blk + k + 1))
                    o = x1l[:, :, bass.ds(i * 4 * CH + k * CH, CH)]
                    nc.vector.tensor_tensor(o, x32[:, k % 2], x1h[:, :, bass.ds(i * 4 * CH + k * CH, CH)],
                                            ALU.subtract).then_inc(x1l_ready, 1)

                for i in rounds(dve, BB // 4):
                    for k in range(4):
                        dve.wait_ge(conv_mm, i * 4 + (BB * blk + k + 1))
                        wait(dve, x1l_ready, i * 4 + (BB * blk + k - 1))
                        cx = ctxb[:, bass.ds(i * 4 * CH + k * CH, CH)].rearrange("p (j g o) -> p j g o", j=1, g=GROUPS)
                        nc.vector.tensor_tensor(x32[:, k % 2].rearrange("p j (g o) -> p j g o", g=GROUPS),
                                                bank[4 + k][:].rearrange("p (g j o) -> p j g o", g=GROUPS, j=J),
                                                cx.broadcast_to([P, J, GROUPS, GC]), ALU.add).then_inc(x32_ready, 1)
                        if k % 2:
                            conv_low(i, k - 1)
                            conv_low(i, k)
                dve.wait_ge(acc_in, 16 * (blk + 1))
                dve.wait_ge(bdn_in, 16 * (blk + 1))
                for t in range(PAIRS):
                    nc.vector.tensor_tensor(acc[:, t], acc[:, t], v[:, 0], ALU.add).then_inc(acc_bias, 1)

                def dequant(i, par, jj, h):
                    s, n = jj % 2, 4 * par + jj
                    half, c = 2 * n + h, slice(h * 512, (h + 1) * 512)
                    if h == 0:
                        wait(dve, w_stored[s], i * 64 + 16 * (n // 2))
                        wait(dve, wl_ready, i * 8 + (n - 1))
                    for m in range(1, NTM):
                        dve.wait_ge(term_ready, i * (16 * NTM) + (NTM * half + m + 1))
                        if m > 1:
                            dve.wait_ge(term_added, i * (16 * STT) + (STT * half + m - 1))
                        nc.vector.scalar_tensor_tensor(out=v[:, s, c], in0=term[:, 0] if m == 1 else v[:, s, c],
                                                       scalar=TERMS[m - 1][2] / TERMS[m][2], in1=term[:, m % 2],
                                                       op0=ALU.mult, op1=ALU.add).then_inc(term_added, 1)
                    dve.wait_ge(term_added, i * (16 * STT) + STT * (half + 1))
                    if jj < 2:
                        dve.wait_ge(amu_in[s], i * 32 + (16 * par + 16))
                        vk = v[:, s, c].rearrange("p (k n) -> p k n", n=P)
                        nc.vector.scalar_tensor_tensor(out=vk, in0=vk, scalar=TERMS[-1][2],
                                                       in1=amu[:, s:s + 1].broadcast_to([P, KT // 2, P]), op0=ALU.mult,
                                                       op1=ALU.mult).then_inc(scaled, 1)
                    else:
                        dve.wait_ge(amd_in, i * 64 + (32 * par + 16 * s + 16))
                        nc.vector.scalar_tensor_tensor(out=v[:, s, c], in0=v[:, s, c], scalar=TERMS[-1][2], in1=amd[:, c],
                                                       op0=ALU.mult, op1=ALU.mult).then_inc(scaled, 1)
                    dve.wait_ge(ab_mm, i * 8 + (n + 1))
                    dve.wait_ge(scaled, i * 16 + (half + 1))
                    nc.vector.tensor_tensor(v[:, s, c], v[:, s, c], bank[2 + h][:], ALU.add).then_inc(w_ready, 1)

                def low(i, par, jj):
                    s, n = jj % 2, 4 * par + jj
                    dve.wait_ge(wh_ready, i * 8 + (JOBS * blk + n + 1))
                    hi, lo = (wuh, wul) if jj < 2 else (wdh, wdl)
                    nc.vector.tensor_tensor(lo[:, 2 * par + s], v[:, s], hi[:, 2 * par + s], ALU.subtract).then_inc(wl_ready, 1)

                def hidden_low(i, w):
                    for s in range(2):
                        dve.wait_ge(hh_ready, i * 8 + (2 * (NU * blk + w) + s + 1))
                        nc.vector.tensor_tensor(hl[:, 2 * (w % 2) + s], bank[s][:], hh[:, 2 * (w % 2) + s],
                                                ALU.subtract).then_inc(hl_ready, 1)

                def add_down(i, u, products=range(8)):
                    for o in products:
                        tt, dh = 4 * (u % 2) + o // 2, o % 2
                        dve.wait_ge(dn_mm, i * 32 + (8 * (NU * blk + u) + o + 1))
                        wait(dve, acc_added, i * 32 + (8 * (NU * blk + u - 2) + o + 1))
                        a = acc[:, tt, dh * 512:(dh + 1) * 512]
                        nc.vector.tensor_tensor(a, a, bank[4 + o % 4][:], ALU.add).then_inc(acc_added, 1)

                dve.wait_ge(acc_bias, PAIRS * (blk + 1))
                for jj in range(4):
                    if blk == 0:
                        dequant(0, 0, jj, 0)
                        dequant(0, 0, jj, 1)
                    low(0, 0, jj)
                hidden_low(0, 0)
                for i in rounds(dve, NG // 2):
                    for k in range(4):
                        step = (i, 1) if k < 2 else (i + 1, 0)
                        a, b = (0, 1) if k % 2 == 0 else (2, 3)
                        if blk == 0:
                            dequant(*step, a, 0)
                            dequant(*step, a, 1)
                        low(*step, a)
                        hidden_low(i, k + 1)
                        for h in range(2):
                            add_down(i, k, range(4 * h, 4 * h + 4))
                            if blk == 0:
                                dequant(*step, b, h)
                        low(*step, b)
                hidden_low(NG // 2, 1)
                add_down(NG // 2, 0)
                add_down(NG // 2, 1)

                dve.wait_ge(dn_mm, 8 * NU * (blk + 1))
                nc.vector.memset(bdg[:], 0.0).then_inc(bdg_zero, 1)
                if blk == 0:
                    dve.wait_ge(mlp_mm, 3)
                    nc.vector.reduce_max(satt[:, 2 * E + 2:2 * E + 3], bank[2][0:B, 0:E], AX.X).then_inc(mlp_dve, 1)
                    dve.wait_ge(mlp_dve, 1)
                    nc.vector.tensor_scalar(satt[:, 2 * E:2 * E + 1], satt[:, 2 * E + 2:2 * E + 3], -1.0, None,
                                            ALU.mult).then_inc(mlp_dve, 1)
                    dve.wait_ge(mlp_act, 3)
                    nc.vector.reciprocal(satt[:, 2 * E + 3:2 * E + 4], satt[:, 2 * E + 1:2 * E + 2]).then_inc(mlp_dve, 1)
                    dve.wait_ge(mlp_dve, 3)
                    nc.vector.tensor_scalar(satt[:, E:2 * E], satt[:, 0:E], satt[:, 2 * E + 3:2 * E + 4], None,
                                            ALU.mult).then_inc(mlp_dve, 1)
                    dve.wait_ge(mlp_mm, 4)
                    nc.vector.tensor_copy(att_t[:], bank[3][0:E, 0:B]).then_inc(att_ready, 1)
                dve.wait_ge(agg_mm, blk + 1)
                for h in range(2):
                    nc.vector.tensor_copy(agg[:, h * 32:(h + 1) * 32], bank[4 + h][:].rearrange("p (o b) -> p o b", b=BB)).then_inc(agg_ready, 1)
                bias_ps = bank[6][:, 0:BB].rearrange("p (q c) -> p q c", c=2)
                for c in range(2):
                    nc.vector.tensor_copy(aggb[64 * c:64 * c + 64, :], bias_ps[64 * c:64 * c + 64, :, c]).then_inc(agg_ready, 1)
                dve.wait_ge(agg_ready, 4 * (blk + 1))
                dve.wait_ge(bdg_zero, blk + 1)

                for i in rounds(dve, PAIRS // 2):
                    for k in range(2):
                        wait(dve, z_mm, i * 2 + (PAIRS * blk + k - 1))
                        for c in range(2):
                            src = agg[64 * c:64 * c + 64, :, bass.ds(i * 4 + (2 * k + c), 1)].rearrange("p o b -> p (o b)")
                            nc.vector.tensor_copy(bdg[64 * c:64 * c + 64, k, 64 * c:64 * c + 64], src).then_inc(bdg_ready, 1)
                        dve.wait_ge(z_tr, i * 2 + (PAIRS * blk + k + 1))
                        wait(dve, gate_mm, i * 2 + (PAIRS * blk + k - 1))
                        for h in range(2):
                            nc.vector.tensor_copy(zt[:, k, h * 512:(h + 1) * 512], bank[4 + h][:]).then_inc(zt_ready, 1)
                        dve.wait_ge(gate_mm, i * 2 + (PAIRS * blk + k + 1))
                        nc.vector.tensor_copy(logits[:, bass.ds(i * 2 + (PAIRS * blk + k), 1)],
                                              bank[6 + k][:, 0:E].rearrange("p (a e) -> p a e", a=1)).then_inc(logit_ready, 1)

            step = [0]

            def link(ins):
                step[0] += 1
                ins.then_inc(route_dve, 1)
                dve.wait_ge(route_dve, step[0])

            dve.wait_ge(logit_ready, TILES)
            for k in range(2):
                dve.wait_ge(z_stored[k], 16 * TILES // 2)
            dve.wait_ge(x_stored, 32)
            dve.wait_ge(iotas, 5)
            for t in range(TILES):
                ins = nc.vector.max(top[:, t], logits[:, t])
            link(ins)
            for t in range(TILES):
                ins = nc.vector.max_index(topi[:, t], top[:, t], logits[:, t])
            link(ins)
            nc.vector.tensor_copy(iota_sf[:], iota_s[:])
            nc.vector.tensor_copy(iota_ef[:], iota_e[:])
            link(nc.vector.tensor_copy(eid[:], topi[:, :, 0]))
            link(nc.vector.tensor_tensor(oh[:], eid[:].rearrange("p (t o) -> p t o", o=1).broadcast_to([P, TILES, E]),
                                         iota_ef[:].rearrange("p (o e) -> p o e", o=1).broadcast_to([P, TILES, E]), ALU.is_equal))
            link(nc.vector.memset(run[:, 0], 0.0))
            dve.wait_ge(route_mm, 1)
            total = bank[1][:, 0:P].rearrange("p (t e) -> p t e", e=E)
            for t in range(TILES):
                link(nc.vector.tensor_tensor(run[:, t + 1], run[:, t], total[:, t], ALU.add))
            link(nc.vector.tensor_scalar(cnt[:], run[:, TILES], float(ST - 1), None, ALU.add))
            link(nc.vector.tensor_single_scalar(cnt2[:], cnt[:], ST.bit_length() - 1, ALU.arith_shift_right))
            link(nc.vector.tensor_copy(ntl[:], cnt2[:]))
            link(nc.vector.memset(end[:, 0:1], 0.0))
            for e in range(E):
                link(nc.vector.tensor_tensor(end[:, e + 1:e + 2], end[:, e:e + 1], ntl[:, e:e + 1], ALU.add))
            link(nc.vector.tensor_tensor(place[:], bank[0][:, 0:P].rearrange("p (t e) -> p t e", e=E), run[:, 0:TILES], ALU.add))
            link(nc.vector.scalar_tensor_tensor(out=place[:], in0=end[:, 0:E].rearrange("p (o e) -> p o e", o=1).broadcast_to([P, TILES, E]),
                                                scalar=float(ST), in1=place[:], op0=ALU.mult, op1=ALU.add))
            link(nc.vector.tensor_tensor(place[:], place[:], oh[:], ALU.mult))
            link(nc.vector.reduce_sum(slotf[:], place[:], AX.X))
            link(nc.vector.tensor_copy(sloti[:, 0], slotf[:]))
            nc.vector.tensor_single_scalar(sloti[:, 1], sloti[:, 0], P - 1, ALU.bitwise_and)
            link(nc.vector.tensor_single_scalar(sloti[:, 2], sloti[:, 0], P.bit_length() - 1, ALU.arith_shift_right))
            link(nc.vector.tensor_copy(slotp[:], sloti[:, 1:3]))
            nc.vector.scalar_tensor_tensor(out=sloti[:, 3], in0=slotp[:, 0], scalar=float(SC), in1=slotp[:, 1], op0=ALU.mult,
                                           op1=ALU.add).then_inc(slots_ready, 1)
            link(nc.vector.tensor_tensor(past[:], end[:, 1:E + 1].rearrange("p (o e) -> p o e", o=1).broadcast_to([P, 16, E]),
                                         iota_sf[:].rearrange("p (s o) -> p s o", o=1).broadcast_to([P, 16, E]), ALU.is_le))
            link(nc.vector.reduce_sum(etf[:], past[:], AX.X))
            nc.vector.tensor_scalar(eti[:], etf[:], float(E - 1), None, ALU.min).then_inc(tiles_ready, 1)

            def chunk_low(i, par, kt):
                dve.wait_ge(whr_ready, i * 16 + (8 * par + kt + 1))
                nc.vector.tensor_tensor(wlr[:, kt % 4], wraw[:, kt], whr[:, kt % 4], ALU.subtract).then_inc(wlr_ready, 1)

            def z_low(i, par):
                for b in range(4):
                    dve.wait_ge(zth_ready, i * 8 + (4 * par + b + 1))
                    nc.vector.tensor_tensor(ztl[:, par, 2 * b:2 * b + 2], bank[4 * par + b][:].rearrange("p (k s) -> p k s", k=2),
                                            zth[:, par, 2 * b:2 * b + 2], ALU.subtract).then_inc(ztl_ready, 1)

            def add_bias(i, par):
                dve.wait_ge(eb_in[par], i * 16 + 16)
                dve.wait_ge(zx_in[par], i * 32 + 32)
                a = zx[:, par, :, L:2 * L]
                nc.vector.tensor_tensor(a, a, ebs[:, par:par + 1].broadcast_to([P, 2, L]), ALU.add).then_inc(xb_ready, 1)

            def add_rows(i, par):
                wait(dve, chunk_mm, i * 16 + (8 * par + 8))
                dve.wait_ge(xb_ready, i * 2 + (par + 1))
                for b in range(4):
                    a = zx[:, par, b // 2, L + (b % 2) * 512:L + (b % 2 + 1) * 512]
                    nc.vector.tensor_tensor(a, a, bank[4 * par + b][:], ALU.add).then_inc(y_ready, 1)

            def expert(i, par, nxt, last):
                for kt in range(KT):
                    chunk_low(i, par, kt)
                    if kt == 0 and last:
                        add_rows(*last)
                    if kt == 3:
                        add_bias(i, par)
                    if kt == 5 and nxt:
                        z_low(*nxt)

            z_low(0, 0)
            for i in rounds(dve, NS // 2):
                expert(i, 0, (i, 1), (i - 1, 1) if not isinstance(i, int) else None)
                expert(i, 1, (i + 1, 0), (i, 0))
            expert(NS // 2, 0, None, (NS // 2 - 1, 1))
            add_rows(NS // 2, 0)

        @block.tensor
        def _(pe):
            mm = nc.tensor.matmul

            def three(ps, ah, al, bh, bl, first, last):
                mm(ps, ah, bh, start=first, stop=False)
                mm(ps, ah, bl, start=False, stop=False)
                return mm(ps, al, bh, start=False, stop=last)

            pe.wait_ge(ident_ready, 2)
            pe.wait_ge(ones_ready, 1)
            for blk in range(BLKS):
                pe.wait_ge(cprod_ready, blk + 1)
                for h in range(2):
                    mm(bank[h][:], ones[:], cprod[:, h * 8:(h + 1) * 8], start=True, stop=False)
                    ins = mm(bank[h][:], ones[0:1, :], cbias[:].rearrange("p (b o) -> p b o", b=1).broadcast_to([1, 8, CH]),
                             start=False, stop=True)
                ins.then_inc(ctx_mm, 1)
                for i in rounds(pe, BB // 4):
                    for k in range(4):
                        if k % 2 == 0:
                            pe.wait_ge(xcv_in[k // 2], i * 16 + (16 * PAIRS // 2 * blk + 16))
                        wait(pe, x32_ready, i * 4 + (BB * blk + k - 3))
                        for g in range(GROUPS):
                            for d in range(2):
                                ins = mm(bank[4 + k][:, g * P:(g + 1) * P], xcv[:, k // 2, k % 2, g, d:d + P], tz[:, d, g],
                                         start=d == 0, stop=d == 1)
                        ins.then_inc(conv_mm, 1)

                def lora_product(i, par, jj):
                    s, n = jj % 2, 4 * par + jj
                    if jj < 2:
                        pe.wait_ge(lora_in[s], i * 64 + (32 * par + 32))
                    wait(pe, w_ready, i * 16 + 2 * n)
                    for h in range(2):
                        if jj < 2:
                            for q in range(4):
                                ins = mm(bank[2 + h][:, q * P:(q + 1) * P], lora[0:R, (4 * h + q) * P:(4 * h + q + 1) * P],
                                         lora_t[0:R, s], start=True, stop=True)
                        else:
                            ins = mm(bank[2 + h][:], lora_t[32:32 + R, s], lora[32:32 + R, h * 512:(h + 1) * 512],
                                     start=True, stop=True)
                    ins.then_inc(ab_mm, 1)

                def up(i, w):
                    half, par = w % 2, (w // 2) % 2
                    pe.wait_ge(wl_ready, i * 8 + (JOBS * blk + 4 * (w // 2) + 2))
                    wait(pe, hl_ready, i * 8 + 2 * (NU * blk + w))
                    t0 = half * HALF
                    for s in range(2):
                        for kt in range(KT):
                            c = slice(kt * P, (kt + 1) * P)
                            ins = three(bank[s][:], wuh[:, 2 * par + s, c], wul[:, 2 * par + s, c], x1h[:, kt, t0:t0 + HALF],
                                        x1l[:, kt, t0:t0 + HALF], kt == 0, kt == KT - 1)
                    ins.then_inc(up_mm, 1)

                def down(i, u):
                    par, hp = (u // 2) % 2, u % 2
                    pe.wait_ge(wl_ready, i * 8 + (JOBS * blk + 4 * (u // 2) + 4))
                    pe.wait_ge(hl_ready, i * 8 + (2 * (NU * blk + u) + 2))
                    for o in range(8):
                        tt, dh = o // 2, o % 2
                        wait(pe, acc_added, i * 32 + (8 * (NU * blk + u) + o - 3))
                        c, d = slice(tt * P, (tt + 1) * P), slice(dh * 512, (dh + 1) * 512)
                        for s in range(2):
                            ins = three(bank[4 + o % 4][:], hh[:, 2 * hp + s, c], hl[:, 2 * hp + s, c], wdh[:, 2 * par + s, d],
                                        wdl[:, 2 * par + s, d], s == 0, s == 1)
                        ins.then_inc(dn_mm, 1)

                pe.wait_ge(x1l_ready, BB * (blk + 1))
                pe.wait_ge(ffn_const, 48 * (blk + 1))
                if blk == 0:
                    for jj in range(4):
                        lora_product(0, 0, jj)
                up(0, 0)
                for i in rounds(pe, NG // 2):
                    for k in range(4):
                        step = (i, 1) if k < 2 else (i + 1, 0)
                        a, b = (0, 1) if k % 2 == 0 else (2, 3)
                        if blk == 0:
                            lora_product(*step, a)
                        up(i, k + 1)
                        down(i, k)
                        if blk == 0:
                            lora_product(*step, b)
                up(NG // 2, 1)
                down(NG // 2, 0)
                down(NG // 2, 1)

                pe.wait_ge(acc_added, 8 * NU * (blk + 1))
                pe.wait_ge(dyn_const, 16 * (CONSTS_DYN + 4 * blk))
                if blk == 0:
                    ins = mm(bank[0][:, 0:B], w0s[:], ct2[:], start=True, stop=True)
                    ins.then_inc(mlp_mm, 1)
                    pe.wait_ge(mlp_act, 1)
                    mm(bank[1][:, 0:B], w1s[:], hid1[:], start=True, stop=True).then_inc(mlp_mm, 1)
                    pe.wait_ge(mlp_act, 2)
                    mm(bank[2][0:B, 0:E], hid2[:], w2s[:], start=True, stop=False)
                    mm(bank[2][0:B, 0:E], ones[0:1, 0:B], b2s[:], start=False, stop=True).then_inc(mlp_mm, 1)
                    pe.wait_ge(mlp_dve, 4)
                    nc.tensor.transpose(bank[3][0:E, 0:B], satt[:, E:2 * E], ident[0:B, 0:B]).then_inc(mlp_mm, 1)
                    pe.wait_ge(att_ready, 1)
                att = att_t[:, BB * blk:BB * (blk + 1)]
                for o in range(CH):
                    mm(bank[4 + o // 32][:, (o % 32) * BB:(o % 32 + 1) * BB], kerns[:, o], att, start=True, stop=True)
                mm(bank[6][:, 0:BB], kernb[:], att, start=True, stop=True).then_inc(agg_mm, 1)

                for i in rounds(pe, PAIRS // 2):
                    for k in range(2):
                        pe.wait_ge(bdg_ready, i * 4 + (2 * PAIRS * blk + 2 * k + 2))
                        wait(pe, z_ready, i * 4 + (2 * PAIRS * blk + 2 * k - 2))
                        for h in range(2):
                            rows = acc[:, bass.ds(i * 2 + k, 1), h * 512:(h + 1) * 512].rearrange("p a l -> p (a l)")
                            ins = mm(bank[2 * k + h][:], bdg[:, k], rows, start=True, stop=True)
                        ins.then_inc(z_mm, 1)
                        pe.wait_ge(z_ready, i * 4 + (2 * PAIRS * blk + 2 * k + 2))
                        wait(pe, zt_ready, i * 4 + (2 * PAIRS * blk + 2 * k))
                        for kt in range(KT):
                            ins = nc.tensor.transpose(bank[4 + kt // 4][:, (kt % 4) * P:(kt % 4 + 1) * P],
                                                      z32[:, k, kt * P:(kt + 1) * P], ident[:])
                        ins.then_inc(z_tr, 1)
                        pe.wait_ge(zt_ready, i * 4 + (2 * PAIRS * blk + 2 * k + 2))
                        wait(pe, logit_ready, i * 2 + (PAIRS * blk + k - 1))
                        mm(bank[6 + k][:, 0:E], ones[0:1, :], gbs[:], start=True, stop=False)
                        for kt in range(KT):
                            ins = mm(bank[6 + k][:, 0:E], zt[:, k, kt * P:(kt + 1) * P], gts[:, kt], start=False, stop=kt == KT - 1)
                        ins.then_inc(gate_mm, 1)

            pe.wait_ge(route_dve, ONEHOT)
            pe.wait_ge(iotas, 5)
            mm(bank[0][:, 0:P], tri[:], oh[:].rearrange("p t e -> p (t e)"), start=True, stop=True)
            mm(bank[1][:, 0:P], ones[:], oh[:].rearrange("p t e -> p (t e)"), start=True, stop=True).then_inc(route_mm, 1)
            pe.wait_ge(slots_ready, 1)

            def rows_transposed(i, par):
                pe.wait_ge(zx_in[par], i * 32 + 32)
                wait(pe, y_ready, i * 8 + (4 * par - 4))
                for b in range(4):
                    for q in range(4):
                        kt, h = 2 * b + q // 2, q % 2
                        ins = nc.tensor.transpose(bank[4 * par + b][:, q * P:(q + 1) * P], zx[:, par, h, kt * P:(kt + 1) * P], ident[:])
                    ins.then_inc(tr_mm, 1)

            def chunk(i, par, kt):
                pe.wait_ge(wlr_ready, i * 16 + (8 * par + kt + 1))
                if kt == 0:
                    pe.wait_ge(ztl_ready, i * 8 + (4 * par + 4))
                for b in range(4):
                    s, d = slice((b // 2) * P, (b // 2 + 1) * P), slice((b % 2) * 512, (b % 2 + 1) * 512)
                    ins = three(bank[4 * par + b][:], zth[:, par, kt, s], ztl[:, par, kt, s], whr[:, kt % 4, d], wlr[:, kt % 4, d],
                                kt == 0, kt == KT - 1)
                ins.then_inc(chunk_mm, 1)

            def expert(i, par, nxt):
                for kt in range(KT):
                    chunk(i, par, kt)
                    if kt == 3 and nxt:
                        rows_transposed(*nxt)

            rows_transposed(0, 0)
            for i in rounds(pe, NS // 2):
                expert(i, 0, (i, 1))
                expert(i, 1, (i + 1, 0))
            expert(NS // 2, 0, None)


def layouts(x, cond_128, fside_S_0, L0_cond_weight, L0_cond_c_weight, L0_ffn_w_up_codes, L0_ffn_w_up_absmax,
            L0_ffn_b_up, L0_ffn_w_up_lora_a, L0_ffn_w_up_lora_b, L0_ffn_w_down_codes, L0_ffn_w_down_absmax, L0_ffn_b_down,
            L0_ffn_w_down_lora_a, L0_ffn_w_down_lora_b, L1_cond_W0, L1_cond_b0, L1_cond_W1, L1_cond_b1, L1_cond_W2,
            L1_cond_b2, L1_cond_weight, L1_cond_bias_k, L1_ffn_gate_w, L1_ffn_gate_b, L1_ffn_expert_w, L1_ffn_expert_b):
    def padded(a, axis, size):
        room = [(0, 0)] * a.ndim
        room[axis] = (0, size - a.shape[axis])
        return np.pad(a, room)

    half = TAPS // 2
    xp = np.pad(x, ((0, 0), (0, 0), (half, J * MB - L - half)))
    x_conv = xp.reshape(B, GROUPS, GC, MB, J).transpose(2, 4, 0, 1, 3).reshape(P, B, GROUPS, MB)
    w = L0_cond_weight.reshape(GROUPS, GC, GC, TAPS)
    toep = np.zeros((GC, J, 2, GROUPS, J, GC), w.dtype)
    for d in range(2):
        for jp in range(J):
            for j in range(J):
                tap = J * d + jp - j
                if 0 <= tap < TAPS:
                    toep[:, jp, d, :, j, :] = w[:, :, :, tap].transpose(2, 0, 1)
    cu = padded(L0_ffn_w_up_codes.reshape(HID, P, J), 0, NT * P).reshape(NT, P, P, J).transpose(0, 2, 3, 1)
    cd = padded(L0_ffn_w_down_codes.reshape(L, HID).T, 0, NT * P).reshape(NT, P, L)
    au = padded(L0_ffn_w_up_absmax.reshape(HID, 16), 0, NT * P).reshape(NT, P, 16).transpose(0, 2, 1)
    ad = padded(L0_ffn_w_down_absmax.reshape(L, HID // 64).T, 0, 2 * NT).reshape(NT, 2, L)
    kern = L1_cond_weight[..., 0]
    return dict(
        x_nat=x.reshape(N, L), x_conv=x_conv, toep=toep.reshape(P, 2, GROUPS, P), cond_t=cond_128.T,
        ctx_w_t=L0_cond_c_weight.T, chan_bias=fside_S_0.reshape(1, CH), codes_up=cu.reshape(NT, P, L), codes_dn=cd,
        am_up=au, am_dn=ad, bias_up=padded(L0_ffn_b_up, 0, NT * P).reshape(NT, P).T, bias_dn=L0_ffn_b_down.reshape(1, L),
        lora_up_at=L0_ffn_w_up_lora_a.reshape(P, J, R).transpose(2, 1, 0).reshape(R, L),
        lora_up_b=padded(L0_ffn_w_up_lora_b, 1, NT * P).reshape(R, NT, P).transpose(1, 0, 2),
        lora_dn_at=padded(L0_ffn_w_down_lora_a, 0, NT * P).reshape(NT, P, R).transpose(0, 2, 1),
        lora_dn_b=L0_ffn_w_down_lora_b, w0=L1_cond_W0, b0=L1_cond_b0.reshape(P, 1), w1=L1_cond_W1,
        b1=L1_cond_b1.reshape(P, 1), w2=L1_cond_W2, b2=L1_cond_b2.reshape(1, E),
        kern=np.concatenate([kern, kern], 2), kern_b=np.concatenate([L1_cond_bias_k] * 2, 1),
        gate_t=L1_ffn_gate_w.T.reshape(KT, P, E).transpose(1, 0, 2), gate_b=L1_ffn_gate_b.reshape(1, E),
        exp_w=L1_ffn_expert_w.transpose(0, 2, 1).reshape(E, KT, P, L).transpose(0, 2, 1, 3), exp_b=L1_ffn_expert_b)


def kernel(**inputs):
    import concourse.bacc as bacc
    from concourse.bass_utils import run_bass_kernel_spmd

    arrays = {name: np.ascontiguousarray(a) for name, a in layouts(**{k: np.asarray(a) for k, a in inputs.items()}).items()}
    nc = bacc.Bacc("TRN2", target_bir_lowering=False, num_devices=1)
    args = {name: nc.dram_tensor(name, a.shape, mybir.dt.from_np(a.dtype), kind="ExternalInput").ap()
            for name, a in arrays.items()}
    out = nc.dram_tensor("out", (N, L), F32, kind="ExternalOutput").ap()
    program(nc, out=out, **args)
    result = run_bass_kernel_spmd(nc, [arrays], core_ids=[0])
    return result.results[0]["out"].reshape(B, CH, L)
```

```python
from contextlib import ExitStack

import concourse.bass as bass
import numpy as np
from concourse import mybir

F32 = mybir.dt.float32
F32R = mybir.dt.float32r
I32 = mybir.dt.int32
U32 = mybir.dt.uint32
ALU = mybir.AluOpType
ACT = mybir.ActivationFunctionType
AX = mybir.AxisListType

P = 128
B, CH, L = 32, 64, 1024
GROUPS, TAPS = 4, 9
GC = CH // GROUPS
J = P // GC
MB = L // J + 1
N = B * CH
BLKS = 2
NB = N // BLKS
BB = B // BLKS
HID = 2752
NT = -(-HID // P)
NG = NT // 2
HALF = 512
ROUNDS = NG // 2
AHEAD = 6
NU = 2 * NG
JOBS = 4 * NG
KT = L // P
R = 16
E = 8
PAIRS = BB // 2
TILES = N // P
ST = 256
NS = (N + E * (ST - 1)) // ST
SC = NS * ST // P
ONEHOT = 4

NF4 = np.array([-1.0, -0.6961928009986877, -0.5250730514526367, -0.39491748809814453, -0.28444138169288635,
                -0.18477343022823334, -0.09105003625154495, 0.0, 0.07958029955625534, 0.16093020141124725,
                0.24611230194568634, 0.33791524171829224, 0.44070982933044434, 0.5626170039176941,
                0.7229568362236023, 1.0], np.float32)


def nf4_terms():
    f, terms = NF4.astype(np.float64), []
    for sign, near in ((1, 8), (-1, 7)):
        slope = base = 0.0
        side = []
        for n in range(4):
            c = near + 2 * sign * n
            new_slope = sign * (f[c + sign] - f[c])
            new_base = f[c] - new_slope * c
            side.append((sign, float(sign * (new_slope - slope)), float((base - new_base) / (new_slope - slope))))
            slope, base = new_slope, new_base
        terms += side[::-1]
    return terms


def wait(eng, sem, value):
    if isinstance(value, int) and value <= 0:
        return
    eng.wait_ge(sem, value)


def rounds(eng, n, last=False):
    yield 0
    with eng.Fori(1, n - last) as i:
        yield i
    if last:
        yield n - 1


def stage_jobs(i, k):
    if isinstance(i, int) and i == ROUNDS - 1 and k == 3:
        return ()
    return (i, 6 + 2 * k), (i, 7 + 2 * k)


def program(nc, x_nat, x_conv, toep, cond_t, ctx_w_t, chan_bias, codes_up, codes_dn, am_up, am_dn, bias_up, bias_dn,
            lora_up_at, lora_up_b, lora_dn_at, lora_dn_b, w0, b0, w1, b1, w2, b2, kern, kern_b, gate_t, gate_b,
            exp_w, exp_b, out):
    TERMS = nf4_terms()
    NHEAD = 3
    CHAIN = TERMS[NHEAD:]
    NCH = len(CHAIN)
    ctx = ExitStack()
    with ctx:
        def sem(name):
            return ctx.enter_context(nc.semaphore(name))

        def sb(stack, name, shape, dt=F32):
            return stack.enter_context(nc.sbuf_tensor(name, shape, dt))

        w_dram = nc.dram_tensor("w_dequantised", (JOBS, P, L), F32, kind="Internal").ap()
        zx_dram = nc.dram_tensor("z_and_x_rows", (N, 2 * L), F32, kind="Internal").ap()
        slot_dram = nc.dram_tensor("slot_token", (P * SC, 1), I32, kind="Internal").ap()

        ident = sb(ctx, "ident", [P, P])
        ones = sb(ctx, "ones", [P, P])
        att_t = sb(ctx, "att_t", [E, B])
        logits = sb(ctx, "logits", [P, TILES, E])

        late = ExitStack()
        acc = sb(late, "acc", [P, PAIRS, L])
        x1h = sb(late, "x1h", [P, KT, NB], F32R)
        x1l = sb(late, "x1l", [P, KT, NB], F32R)

        ffn = ExitStack()
        low_parts = ExitStack()
        wul = sb(low_parts, "wul", [P, 4, L], F32R)
        wdl = sb(low_parts, "wdl", [P, 4, L], F32R)
        low_parts.close()
        wu = sb(ffn, "wu", [P, 4, L])
        wd = sb(ffn, "wd", [P, 4, L])
        wuh = sb(ffn, "wuh", [P, 4, L], F32R)
        wdh = sb(ffn, "wdh", [P, 4, L], F32R)
        hh = sb(ffn, "hh", [P, 4, HALF], F32R)
        hl = sb(ffn, "hl", [P, 4, HALF], F32R)
        term = sb(ffn, "term", [P, 2, L])
        hterm = sb(ffn, "hterm", [P, L])
        codes = sb(ffn, "codes", [P, 2, L], I32)
        am = sb(ffn, "am", [P, L])
        lora = sb(ffn, "lora", [48, L])
        lora_t = sb(ffn, "lora_t", [48, 2, P])
        bup = sb(ffn, "bup", [P, NT])
        ffn.close()

        conv = ExitStack()
        xcv = sb(conv, "xcv", [P, 2, 2, GROUPS, MB])
        tz = sb(conv, "tz", [P, 2, GROUPS, P])
        ct = sb(conv, "ct", [P, B])
        cwt = sb(conv, "cwt", [P, CH])
        cbias = sb(conv, "cbias", [1, CH])
        cprod = sb(conv, "cprod", [P, BB, CH])
        ctxb = sb(conv, "ctxb", [P, NB])
        x32 = sb(conv, "x32", [P, 2, KT, CH])
        bdn = sb(conv, "bdn", [P, L])
        conv.close()

        dyn = ExitStack()
        ct2 = sb(dyn, "ct2", [P, B])
        w0s = sb(dyn, "w0s", [P, P])
        w1s = sb(dyn, "w1s", [P, P])
        w2s = sb(dyn, "w2s", [P, E])
        b0s = sb(dyn, "b0s", [P, 1])
        b1s = sb(dyn, "b1s", [P, 1])
        b2s = sb(dyn, "b2s", [1, E])
        hid1 = sb(dyn, "hid1", [P, B])
        hid2 = sb(dyn, "hid2", [P, B])
        satt = sb(dyn, "satt", [B, 3 * E])
        kerns = sb(dyn, "kerns", [E, CH, P])
        kernb = sb(dyn, "kernb", [E, P])
        gts = sb(dyn, "gts", [P, KT, E])
        gbs = sb(dyn, "gbs", [1, E])
        agg = sb(dyn, "agg", [P, CH, BB])
        aggb = sb(dyn, "aggb", [P, PAIRS])
        bdg = sb(dyn, "bdg", [P, 2, P])
        z32 = sb(dyn, "z32", [P, 2, L])
        zt = sb(dyn, "zt", [P, 2, L])
        dyn.close()
        late.close()

        moe = ExitStack()
        whr = sb(moe, "whr", [P, 4, L], F32R)
        wlr = sb(moe, "wlr", [P, 4, L], F32R)
        zth = sb(moe, "zth", [P, 2, KT, ST], F32R)
        ztl = sb(moe, "ztl", [P, 2, KT, ST], F32R)
        wraw = sb(moe, "wraw", [P, KT, L])
        zx = sb(moe, "zx", [P, 2, 2, 2 * L])
        ebs = sb(moe, "ebs", [P, 2, L])
        tri = sb(moe, "tri", [P, P])
        top = sb(moe, "top", [P, TILES, E])
        topi = sb(moe, "topi", [P, TILES, E], U32)
        eid = sb(moe, "eid", [P, TILES])
        iota_e = sb(moe, "iota_e", [P, E], I32)
        iota_ef = sb(moe, "iota_ef", [P, E])
        iota_s = sb(moe, "iota_s", [P, 16], I32)
        iota_sf = sb(moe, "iota_sf", [P, 16])
        oh = sb(moe, "oh", [P, TILES, E])
        run = sb(moe, "run", [P, TILES + 1, E])
        cnt = sb(moe, "cnt", [P, E], I32)
        cnt2 = sb(moe, "cnt2", [P, E], I32)
        ntl = sb(moe, "ntl", [P, E])
        end = sb(moe, "end", [P, E + 1])
        place = sb(moe, "place", [P, TILES, E])
        slotf = sb(moe, "slotf", [P, TILES])
        sloti = sb(moe, "sloti", [P, 4, TILES], I32)
        slotp = sb(moe, "slotp", [P, 2, TILES])
        tokid = sb(moe, "tokid", [P, TILES], I32)
        nobody = sb(moe, "nobody", [P, SC], I32)
        table = sb(moe, "table", [P, SC], I32)
        past = sb(moe, "past", [P, 16, E])
        etf = sb(moe, "etf", [P, 16])
        eti = sb(moe, "eti", [P, 16], I32)
        ridx = sb(moe, "ridx", [P, 4], I32)
        moe.close()

        pair = [ctx.enter_context(nc.psum_tensor(f"pair{i}", [P, 1024], F32)) for i in range(4)]
        bank = [pair[i // 2][:, i % 2 * 512:(i % 2 + 1) * 512] for i in range(8)]

        ident_ready, ones_ready = sem("ident_ready"), sem("ones_ready")
        conv_const = sem("conv_const")
        xcv_in = [sem(f"xcv_in{i}") for i in range(2)]
        acc_in, bdn_in = sem("acc_in"), sem("bdn_in")
        cprod_ready, ctx_mm, ctxb_ready = sem("cprod_ready"), sem("ctx_mm"), sem("ctxb_ready")
        conv_mm, x32_ready, x1h_ready, x1l_ready = sem("conv_mm"), sem("x32_ready"), sem("x1h_ready"), sem("x1l_ready")
        acc_bias = sem("acc_bias")
        ffn_const = sem("ffn_const")
        codes_in = [sem(f"codes_in{i}") for i in range(2)]
        am_in = sem("am_in")
        lora_in = [sem(f"lora_in{i}") for i in range(2)]
        head_terms, head_added = sem("head_terms"), sem("head_added")
        term_ready, term_added, scaled, ab_mm, w_ready = (sem(n) for n in (
            "term_ready", "term_added", "scaled", "ab_mm", "w_ready"))
        w_stored = [sem(f"w_stored{i}") for i in range(2)]
        w_in = [sem(f"w_in{i}") for i in range(8)]
        wh_ready, wl_ready = sem("wh_ready"), sem("wl_ready")
        up_mm, relu_done, hh_ready, hl_ready = sem("up_mm"), sem("relu_done"), sem("hh_ready"), sem("hl_ready")
        dn_mm, acc_added = sem("dn_mm"), sem("acc_added")
        dyn_const, mlp_mm, mlp_act, mlp_dve, att_ready = (sem(n) for n in (
            "dyn_const", "mlp_mm", "mlp_act", "mlp_dve", "att_ready"))
        agg_mm, agg_ready, bdg_zero, bdg_ready = sem("agg_mm"), sem("agg_ready"), sem("bdg_zero"), sem("bdg_ready")
        z_mm, z_ready, z_tr, zt_ready, gate_mm, logit_ready = (sem(n) for n in (
            "z_mm", "z_ready", "z_tr", "zt_ready", "gate_mm", "logit_ready"))
        z_stored = [sem(f"z_stored{i}") for i in range(2)]
        x_stored = sem("x_stored")
        iotas, nobody_ready, table_clear, table_set, table_in = (sem(n) for n in (
            "iotas", "nobody_ready", "table_clear", "table_set", "table_in"))
        route_dve, route_mm, slots_ready, tiles_ready = (sem(n) for n in (
            "route_dve", "route_mm", "slots_ready", "tiles_ready"))
        zx_zero, ridx_ready = sem("zx_zero"), sem("ridx_ready")
        zx_in = [sem(f"zx_in{i}") for i in range(2)]
        wraw_in = [sem(f"wraw_in{i}") for i in range(KT)]
        eb_in = [sem(f"eb_in{i}") for i in range(2)]
        whr_ready, wlr_ready, chunk_mm = sem("whr_ready"), sem("wlr_ready"), sem("chunk_mm")
        tr_mm, zth_ready, ztl_ready = sem("tr_mm"), sem("zth_ready"), sem("ztl_ready")
        xb_ready, y_ready = sem("xb_ready"), sem("y_ready")
        out_done = [sem(f"out_done{i}") for i in range(2)]

        act_passed, pool_passed = sem("act_passed"), sem("pool_passed")

        def slot(n):
            return 2 * (n // 4 % 2) + n % 2

        def whole(n):
            return (wu if n % 4 < 2 else wd)[:, slot(n)]

        def high_part(n):
            return (wuh if n % 4 < 2 else wdh)[:, slot(n)]

        def low_part(n):
            return (wul if n % 4 < 2 else wdl)[:, slot(n)]

        def wait_place(eng, i, n, blk):
            before = NU * blk + 2 * (n // 4) - 2
            if n % 4 < 2:
                wait(eng, up_mm, i * 4 + before)
            else:
                wait(eng, dn_mm, i * 16 + 4 * before)

        block = ctx.enter_context(nc.Block())

        CONSTS_DYN = 11

        @block.sync
        def _(sp):
            for blk in range(BLKS):
                wait(sp, logit_ready, PAIRS * blk)
                for k in range(2):
                    wait(sp, z_stored[k], 16 * PAIRS // 2 * blk)
                for dst, src in ((tz[:], toep), (ct[:], cond_t), (cwt[:], ctx_w_t), (cbias[:], chan_bias)):
                    sp.dma_start(dst, src).then_inc(conv_const, 16)
                for i in rounds(sp, PAIRS // 2):
                    for k in range(2):
                        wait(sp, conv_mm, i * 4 + (BB * blk + 2 * k - 2) if not isinstance(i, int) or i else 0)
                        sp.dma_start(xcv[:, k], x_conv[:, bass.ds(i * 4 + (BB * blk + 2 * k), 2)]).then_inc(xcv_in[k], 16)
                    if isinstance(i, int):
                        wait(sp, x_stored, 16 * blk)
                        sp.dma_start(bdn[:], bias_dn[0:1, :].broadcast_to([P, L])).then_inc(bdn_in, 16)
                        sp.dma_start(acc[:], x_nat[blk * NB:(blk + 1) * NB].rearrange("(t p) l -> p t l", p=P)).then_inc(acc_in, 16)
                wait(sp, x1l_ready, BB * (blk + 1))
                wait(sp, acc_bias, PAIRS * (blk + 1))
                sp.dma_start(lora[0:R], lora_up_at).then_inc(ffn_const, 16)
                sp.dma_start(lora[32:32 + R], lora_dn_b).then_inc(ffn_const, 16)
                sp.dma_start(bup[:], bias_up).then_inc(ffn_const, 16)

                def load_scales(i, n):
                    t = i * 4 + (2 * (n // 4) + n % 2)
                    wait(sp, scaled, i * 8 + n)
                    if n % 4 < 2:
                        sp.dma_start(am[:, 0:P].rearrange("p (o n) -> p o n", o=1), am_up[bass.ds(t, 1)].rearrange(
                            "a k (o n) -> (a k) o n", o=1).broadcast_to([16, 8, P])).then_inc(am_in, 16)
                    else:
                        sp.dma_start(am[:], am_dn[bass.ds(t, 1)].rearrange("a k (o n) -> (a k) o n", o=1)
                                     .broadcast_to([2, 64, L])).then_inc(am_in, 16)

                def load(i, n):
                    s, t = n % 2, i * 4 + (2 * (n // 4) + n % 2)
                    if blk == 0:
                        wait(sp, term_ready, i * (8 * NCH) + NCH * (n - 1))
                        src = codes_up if n % 4 < 2 else codes_dn
                        sp.dma_start(codes[:, s], src[bass.ds(t, 1)].rearrange("a p n -> p (a n)")).then_inc(codes_in[s], 16)
                        if not isinstance(i, int) or i * 8 + n > 0:
                            load_scales(i, n - 1)
                        if n % 4 < 2:
                            wait(sp, ab_mm, i * 8 + (n - 1))
                            sp.dma_start(lora_t[0:R, s], lora_up_b[bass.ds(t, 1)].rearrange("a r n -> (a r) n")).then_inc(lora_in[s], 16)
                            sp.dma_start(lora_t[32:32 + R, s], lora_dn_at[bass.ds(t, 1)].rearrange("a r n -> (a r) n")).then_inc(lora_in[s], 16)
                    else:
                        wait_place(sp, i, n, blk)
                        sp.dma_start(whole(n), w_dram[bass.ds(i * 8 + n, 1)].rearrange("a p n -> p (a n)")).then_inc(w_in[n % 8], 16)

                for n in range(AHEAD):
                    load(0, n)
                for i in rounds(sp, ROUNDS, last=True):
                    for k in range(4):
                        for job in stage_jobs(i, k):
                            load(*job)
                if blk == 0:
                    load_scales(0, JOBS - 1)

                wait(sp, dn_mm, 4 * NU * (blk + 1))
                wait(sp, acc_added, 4 * NU * (blk + 1))
                if blk == 0:
                    for dst, src in ((ct2[:], cond_t), (w0s[:], w0), (w1s[:], w1), (w2s[:], w2), (b0s[:], b0), (b1s[:], b1),
                                     (b2s[:], b2)):
                        sp.dma_start(dst, src).then_inc(dyn_const, 16)
                for dst, src in ((kerns[:], kern), (kernb[:], kern_b), (gts[:], gate_t), (gbs[:], gate_b)):
                    sp.dma_start(dst, src).then_inc(dyn_const, 16)

            wait(sp, logit_ready, TILES)
            for k in range(2):
                wait(sp, z_stored[k], 16 * TILES // 2)
            wait(sp, x_stored, 32)
            wait(sp, nobody_ready, 1)
            sp.dma_start(slot_dram.rearrange("(p c) o -> p (c o)", p=P), nobody[:]).then_inc(table_clear, 16)
            wait(sp, table_set, 16 * TILES)
            sp.dma_start(table[:], slot_dram.rearrange("(p c) o -> p (c o)", p=P)).then_inc(table_in, 16)
            wait(sp, tiles_ready, 1)

            def load_expert(i, par):
                e = sp.value_load(eti[0:1, bass.ds(i * 2 + par, 1)], min_val=0, max_val=E - 1)
                for kt in range(KT):
                    wait(sp, wlr_ready, i * 16 + (8 * par + kt - 7))
                    sp.dma_start(wraw[:, kt], exp_w[bass.ds(e, 1), :, kt].rearrange("a p n -> p (a n)")).then_inc(wraw_in[kt], 16)
                wait(sp, xb_ready, i * 2 + (par - 1))
                sp.dma_start(ebs[:, par], exp_b[bass.ds(e, 1)].broadcast_to([P, L])).then_inc(eb_in[par], 16)

            for i in rounds(sp, NS // 2):
                load_expert(i, 0)
                load_expert(i, 1)
            load_expert(NS // 2, 0)

        @block.gpsimd
        def _(pool):
            last_row = pool.to_reg(N - 1)
            nc.gpsimd.memset(ident[:], 0.0).then_inc(ident_ready, 1)
            nc.gpsimd.memset(ones[:], 1.0).then_inc(ones_ready, 1)
            pool.wait_ge(ident_ready, 1)
            nc.gpsimd.affine_select(out=ident[:], in_=ident[:], compare_op=ALU.not_equal, fill=1.0, base=0,
                                    pattern=[[-1, P]], channel_multiplier=1).then_inc(ident_ready, 1)

            def head(i, n, m):
                pool.wait_ge(head_terms, i * (8 * NHEAD) + (NHEAD * n + m + 1))
                if m > 1:
                    pool.wait_ge(head_added, i * 16 + (2 * n + m - 1))
                op = ALU.add if TERMS[m][0] > 0 else ALU.subtract
                nc.gpsimd.tensor_tensor(whole(n), whole(n), hterm[:], op).then_inc(head_added, 1)

            def low(i, n):
                pool.wait_ge(wh_ready, i * 8 + (n + 1))
                pool.wait_ge(w_stored[n % 2], i * 64 + 16 * (n // 2 + 1))
                nc.gpsimd.tensor_tensor(low_part(n), whole(n), high_part(n), ALU.subtract).then_inc(wl_ready, 1)

            def finish(i, n, more=True):
                if more:
                    head(i, n + 1, 1)
                if not isinstance(i, int) or i * 8 + n > 0:
                    low(i, n - 1)
                if more:
                    head(i, n + 1, 2)
                pool.wait_ge(term_added, i * (8 * NCH) + NCH * (n + 1))
                pool.wait_ge(am_in, i * 128 + 16 * (n + 1))
                if n % 4 < 2:
                    w = whole(n).rearrange("p (k n) -> p k n", n=P)
                    scale = am[:, 0:P].rearrange("p (o n) -> p o n", o=1).broadcast_to([P, KT, P])
                else:
                    w, scale = whole(n), am[:]
                nc.gpsimd.tensor_tensor(w, w, scale, ALU.mult).then_inc(scaled, 1)

            for blk in range(BLKS):
                pool.wait_ge(acc_in, 16 * (blk + 1))
                pool.wait_ge(bdn_in, 16 * (blk + 1))
                for t in range(PAIRS):
                    nc.gpsimd.tensor_tensor(acc[:, t], acc[:, t], bdn[:], ALU.add).then_inc(acc_bias, 1)
                if blk == 0:
                    head(0, 0, 1)
                    head(0, 0, 2)
                    for n in range(AHEAD):
                        finish(0, n)
                    for i in rounds(pool, ROUNDS, last=True):
                        for k in range(4):
                            for job in stage_jobs(i, k):
                                finish(*job, more=not isinstance(i, int) or i * 8 + job[1] < JOBS - 1)
                    low(0, JOBS - 1)
                wait(pool, acc_added, 4 * NU * (blk + 1))
                pool.dma_start(zx_dram[blk * NB:(blk + 1) * NB, L:].rearrange("(t p) l -> p t l", p=P), acc[:]).then_inc(x_stored, 16)
                for i in rounds(pool, PAIRS // 2):
                    for k in range(2):
                        wait(pool, z_ready, i * 4 + (2 * PAIRS * blk + 2 * k + 2))
                        pool.dma_start(zx_dram[bass.ds(i * 2 * P + (blk * NB + k * P), P), 0:L], z32[:, k]).then_inc(z_stored[k], 16)

            wait(pool, logit_ready, TILES)
            for k in range(2):
                wait(pool, z_stored[k], 16 * TILES // 2)
            wait(pool, x_stored, 32)
            nc.gpsimd.iota(iota_e[:], [[1, E]], base=0, channel_multiplier=0).then_inc(iotas, 1)
            nc.gpsimd.iota(iota_s[:], [[1, 16]], base=0, channel_multiplier=0).then_inc(iotas, 1)
            nc.gpsimd.iota(tokid[:], [[P, TILES]], base=0, channel_multiplier=1).then_inc(iotas, 1)
            nc.gpsimd.iota(nobody[:], [[0, SC]], base=1 << 20, channel_multiplier=0).then_inc(nobody_ready, 1)
            nc.gpsimd.memset(tri[:], 1.0).then_inc(iotas, 1)
            pool.wait_ge(iotas, 4)
            nc.gpsimd.affine_select(out=tri[:], in_=tri[:], compare_op=ALU.is_gt, fill=0.0, base=0,
                                    pattern=[[1, P]], channel_multiplier=-1).then_inc(iotas, 1)
            nc.gpsimd.memset(zx[:], 0.0).then_inc(zx_zero, 1)
            pool.wait_ge(slots_ready, 1)
            pool.wait_ge(table_clear, 16)
            for t in range(TILES):
                pool.indirect_dma_start(slot_dram, bass.IndirectOffsetOnAxis(sloti[:, 3, t:t + 1], 0),
                                        tokid[:, t:t + 1], None).then_inc(table_set, 16)
            pool.wait_ge(table_in, 16)
            pool.wait_ge(zx_zero, 1)

            def gather(i, par):
                wait(pool, out_done[par], i * 32)
                nc.gpsimd.tensor_copy(ridx[:, 2 * par:2 * par + 2], table[:, bass.ds(i * 4 + 2 * par, 2)]).then_inc(ridx_ready, 1)
                wait(pool, ridx_ready, i * 2 + (par + 1))
                pool.sem_inc(pool_passed, 1)
                for h in range(2):
                    pool.indirect_dma_start(zx[:, par, h], None, zx_dram,
                                            bass.IndirectOffsetOnAxis(ridx[:, 2 * par + h:2 * par + h + 1], 0),
                                            bounds_check=last_row, oob_is_err=False).then_inc(zx_in[par], 16)

            def scatter(i, par):
                wait(pool, y_ready, i * 8 + (4 * par + 4))
                pool.sem_inc(pool_passed, 1)
                for h in range(2):
                    pool.indirect_dma_start(out, bass.IndirectOffsetOnAxis(ridx[:, 2 * par + h:2 * par + h + 1], 0),
                                            zx[:, par, h, L:2 * L], None,
                                            bounds_check=last_row, oob_is_err=False).then_inc(out_done[par], 16)

            gather(0, 0)
            for i in rounds(pool, NS // 2):
                gather(i, 1)
                scatter(i, 0)
                gather(i + 1, 0)
                scatter(i, 1)
            scatter(NS // 2, 0)
            pool.wait_ge(out_done[0], 32 * (NS // 2 + 1))
            pool.wait_ge(out_done[1], 32 * (NS // 2))
            pool.wait_ge(w_stored[0], 16 * JOBS // 2)
            pool.wait_ge(w_stored[1], 16 * JOBS // 2)

        @block.scalar
        def _(act):
            for blk in range(BLKS):
                for i in rounds(act, BB // 4):
                    for k in range(4):
                        act.wait_ge(x32_ready, i * 4 + (BB * blk + k + 1))
                        act.sem_inc(act_passed, 1)
                        nc.scalar.activation(x1h[:, :, bass.ds(i * 4 * CH + k * CH, CH)], x32[:, k % 2], ACT.Copy).then_inc(x1h_ready, 1)

                def look(out, i, n, m):
                    sign, scale, bend = TERMS[m]
                    return nc.scalar.activation(out, codes[:, n % 2], ACT.Relu, scale=scale, bias=-scale * bend)

                def head(i, n, terms):
                    for m in terms:
                        if m == 0:
                            act.wait_ge(codes_in[n % 2], i * 64 + 16 * (n // 2 + 1))
                            wait_place(act, i, n, 0)
                        else:
                            wait(act, head_added, i * 16 + (2 * n + m - 1))
                        look(whole(n) if m == 0 else hterm[:], i, n, m).then_inc(head_terms, 1)

                def chain(i, n, terms):
                    for m in terms:
                        wait(act, term_added, i * (8 * NCH) + (NCH * n + m - 1))
                        look(term[:, (NCH * n + m) % 2], i, n, m + NHEAD).then_inc(term_ready, 1)

                def high(i, n):
                    if blk == 0:
                        act.wait_ge(w_ready, i * 8 + (n + 1))
                        act.dma_start(w_dram[bass.ds(i * 8 + n, 1)].rearrange("a p n -> p (a n)"),
                                      whole(n)).then_inc(w_stored[n % 2], 16)
                    else:
                        act.wait_ge(w_in[n % 8], i * 16 + 16 * (n // 8 + 1))
                    nc.scalar.activation(high_part(n), whole(n), ACT.Copy).then_inc(wh_ready, 1)

                def relu(i, w):
                    act.wait_ge(up_mm, i * 4 + (NU * blk + w + 1))
                    act.sem_inc(act_passed, 1)
                    for s in range(2):
                        nc.scalar.activation(bank[s], bank[s], ACT.Relu,
                                             bias=bup[:, bass.ds(i * 4 + (2 * (w // 2) + s), 1)]).then_inc(relu_done, 1)
                    wait(act, dn_mm, i * 16 + 4 * (NU * blk + w - 1))
                    act.wait_ge(relu_done, i * 8 + 2 * (NU * blk + w + 1))
                    h = 2 * (w % 2)
                    nc.scalar.activation(hh[:, h:h + 2], pair[0][:].rearrange("p (s t) -> p s t", s=2), ACT.Copy).then_inc(hh_ready, 1)

                def prepare(i, n, more=True, unit=None):
                    first = isinstance(i, int) and i * 8 + n == 0
                    if blk == 0:
                        chain(i, n, range(0, 3))
                        if not first:
                            high(i, n - 1)
                        if more:
                            head(i, n + 1, (0, 1))
                        chain(i, n, range(3, 4))
                        if unit:
                            relu(*unit)
                        if more:
                            head(i, n + 1, (2,))
                        chain(i, n, range(4, NCH))
                    else:
                        if not first:
                            high(i, n - 1)
                        if unit:
                            relu(*unit)

                act.wait_ge(ffn_const, 48 * (blk + 1))
                if blk == 0:
                    head(0, 0, (0, 1, 2))
                for n in range(AHEAD):
                    prepare(0, n, unit=(0, 0) if n == 4 else None)
                for i in rounds(act, ROUNDS, last=True):
                    for k in range(4):
                        jobs = stage_jobs(i, k)
                        if jobs:
                            prepare(*jobs[0], unit=(i, k + 1))
                            prepare(*jobs[1], more=not isinstance(i, int) or i * 8 + jobs[1][1] < JOBS - 1)
                        else:
                            high(0, JOBS - 1)
                            relu(i, k + 1)
                relu(ROUNDS, 1)

                if blk == 0:
                    act.wait_ge(dyn_const, 16 * 11)
                    act.wait_ge(mlp_mm, 1)
                    nc.scalar.activation(hid1[:], bank[0][:, 0:B], ACT.Gelu, bias=b0s[:, 0:1]).then_inc(mlp_act, 1)
                    act.wait_ge(mlp_mm, 2)
                    nc.scalar.activation(hid2[:], bank[1][:, 0:B], ACT.Gelu, bias=b1s[:, 0:1]).then_inc(mlp_act, 1)
                    act.wait_ge(mlp_dve, 2)
                    nc.scalar.activation(satt[:, 0:E], bank[2][0:B, 0:E], ACT.Exp, bias=satt[:, 2 * E:2 * E + 1],
                                         accum_out=satt[:, 2 * E + 1:2 * E + 2]).then_inc(mlp_act, 1)
                act.wait_ge(agg_ready, 4 * (blk + 1))
                for i in rounds(act, PAIRS // 2):
                    for k in range(2):
                        act.wait_ge(z_mm, i * 2 + (PAIRS * blk + k + 1))
                        wait(act, z_stored[k], i * 16 + (16 * PAIRS // 2 * blk))
                        wait(act, z_tr, i * 2 + (PAIRS * blk + k - 1))
                        for h in range(2):
                            nc.scalar.activation(z32[:, k, h * 512:(h + 1) * 512], bank[2 * k + h][:], ACT.Identity,
                                                 bias=aggb[:, bass.ds(i * 2 + k, 1)]).then_inc(z_ready, 1)

            def chunk_high(i, par, kt):
                act.wait_ge(wraw_in[kt], i * 32 + (16 * par + 16))
                wait(act, chunk_mm, i * 16 + (8 * par + kt - 3))
                nc.scalar.activation(whr[:, kt % 4], wraw[:, kt], ACT.Copy).then_inc(whr_ready, 1)

            def z_high(i, par):
                for b in range(4):
                    act.wait_ge(tr_mm, i * 8 + (4 * par + b + 1))
                    wait(act, chunk_mm, i * 16 + (8 * par - 8))
                    nc.scalar.activation(zth[:, par, 2 * b:2 * b + 2], bank[4 * par + b][:].rearrange("p (k s) -> p k s", k=2),
                                         ACT.Copy).then_inc(zth_ready, 1)

            def expert(i, par, nxt):
                for kt in range(KT):
                    chunk_high(i, par, kt)
                    if kt == 5 and nxt:
                        z_high(*nxt)

            wait(act, logit_ready, TILES)
            for k in range(2):
                wait(act, z_stored[k], 16 * TILES // 2)
            z_high(0, 0)
            for i in rounds(act, NS // 2):
                expert(i, 0, (i, 1))
                expert(i, 1, (i + 1, 0))
            expert(NS // 2, 0, None)

        @block.vector
        def _(dve):
            for blk in range(BLKS):
                dve.wait_ge(conv_const, 64 * (blk + 1))
                cb = ct[:, BB * blk:BB * (blk + 1)].rearrange("p (b o) -> p b o", o=1).broadcast_to([P, BB, CH])
                cw = cwt[:].rearrange("p (b o) -> p b o", b=1).broadcast_to([P, BB, CH])
                nc.vector.tensor_tensor(cprod[:], cb, cw, ALU.mult).then_inc(cprod_ready, 1)
                dve.wait_ge(ctx_mm, blk + 1)
                for h in range(2):
                    nc.vector.tensor_copy(ctxb[:, h * 512:(h + 1) * 512], bank[h][:]).then_inc(ctxb_ready, 1)
                dve.wait_ge(ctxb_ready, 2 * (blk + 1))

                def conv_low(i, k):
                    dve.wait_ge(x1h_ready, i * 4 + (BB * blk + k + 1))
                    o = x1l[:, :, bass.ds(i * 4 * CH + k * CH, CH)]
                    nc.vector.tensor_tensor(o, x32[:, k % 2], x1h[:, :, bass.ds(i * 4 * CH + k * CH, CH)],
                                            ALU.subtract).then_inc(x1l_ready, 1)

                for i in rounds(dve, BB // 4):
                    for k in range(4):
                        dve.wait_ge(conv_mm, i * 4 + (BB * blk + k + 1))
                        wait(dve, x1l_ready, i * 4 + (BB * blk + k - 1))
                        cx = ctxb[:, bass.ds(i * 4 * CH + k * CH, CH)].rearrange("p (j g o) -> p j g o", j=1, g=GROUPS)
                        nc.vector.tensor_tensor(x32[:, k % 2].rearrange("p j (g o) -> p j g o", g=GROUPS),
                                                bank[4 + k][:].rearrange("p (g j o) -> p j g o", g=GROUPS, j=J),
                                                cx.broadcast_to([P, J, GROUPS, GC]), ALU.add).then_inc(x32_ready, 1)
                        if k % 2:
                            conv_low(i, k - 1)
                            conv_low(i, k)
                def chain(i, n, terms):
                    if not blk:
                        for m in terms:
                            dve.wait_ge(term_ready, i * (8 * NCH) + (NCH * n + m + 1))
                            if m == 0:
                                dve.wait_ge(head_added, i * 16 + 2 * (n + 1))
                            else:
                                dve.wait_ge(term_added, i * (8 * NCH) + (NCH * n + m))
                            op = ALU.add if CHAIN[m][0] > 0 else ALU.subtract
                            nc.vector.tensor_tensor(whole(n), whole(n), term[:, (NCH * n + m) % 2], op).then_inc(term_added, 1)

                def add_lora(i, n):
                    if not blk:
                        dve.wait_ge(ab_mm, i * 8 + (n + 1))
                        dve.wait_ge(scaled, i * 8 + (n + 1))
                        nc.vector.tensor_tensor(whole(n), whole(n), pair[1][:], ALU.add).then_inc(w_ready, 1)

                def low(i, n):
                    if blk:
                        dve.wait_ge(wh_ready, i * 8 + (JOBS * blk + n + 1))
                        nc.vector.tensor_tensor(low_part(n), whole(n), high_part(n), ALU.subtract).then_inc(wl_ready, 1)

                def hidden_low(i, w):
                    dve.wait_ge(hh_ready, i * 4 + (NU * blk + w + 1))
                    h = 2 * (w % 2)
                    nc.vector.tensor_tensor(hl[:, h:h + 2], pair[0][:].rearrange("p (s t) -> p s t", s=2), hh[:, h:h + 2],
                                            ALU.subtract).then_inc(hl_ready, 1)

                def add_down(i, u, j):
                    dve.wait_ge(dn_mm, i * 16 + (4 * (NU * blk + u) + j + 1))
                    wait(dve, acc_added, i * 16 + (4 * (NU * blk + u - 2) + j + 1))
                    a = acc[:, 4 * (u % 2) + j]
                    nc.vector.tensor_tensor(a, a, pair[2 + j % 2][:], ALU.add).then_inc(acc_added, 1)

                dve.wait_ge(acc_bias, PAIRS * (blk + 1))
                for n in range(AHEAD):
                    chain(0, n, range(2))
                    if n:
                        add_lora(0, n - 1)
                        low(0, n - 1)
                    chain(0, n, range(2, NCH))
                    if n == 4:
                        hidden_low(0, 0)
                for i in rounds(dve, ROUNDS, last=True):
                    for k in range(4):
                        jobs = stage_jobs(i, k)
                        if jobs:
                            a, b = jobs
                            chain(*a, range(0, 2))
                            add_lora(i, a[1] - 1)
                            low(i, a[1] - 1)
                            chain(*a, range(2, 4))
                            hidden_low(i, k + 1)
                            add_down(i, k, 0)
                            low(*a)
                            chain(*a, range(4, NCH))
                            chain(*b, range(0, 1))
                            add_down(i, k, 1)
                            chain(*b, range(1, 2))
                            add_lora(*a)
                            chain(*b, range(2, 3))
                            add_down(i, k, 2)
                            chain(*b, range(3, 4))
                            add_down(i, k, 3)
                            chain(*b, range(4, NCH))
                        else:
                            add_lora(0, JOBS - 1)
                            low(0, JOBS - 1)
                            hidden_low(i, k + 1)
                            for j in range(4):
                                add_down(i, k, j)
                for j in range(4):
                    add_down(ROUNDS, 0, j)
                    if j == 0:
                        hidden_low(ROUNDS, 1)
                for j in range(4):
                    add_down(ROUNDS, 1, j)

                dve.wait_ge(dn_mm, 4 * NU * (blk + 1))
                nc.vector.memset(bdg[:], 0.0).then_inc(bdg_zero, 1)
                if blk == 0:
                    dve.wait_ge(mlp_mm, 3)
                    nc.vector.reduce_max(satt[:, 2 * E + 2:2 * E + 3], bank[2][0:B, 0:E], AX.X).then_inc(mlp_dve, 1)
                    dve.wait_ge(mlp_dve, 1)
                    nc.vector.tensor_scalar(satt[:, 2 * E:2 * E + 1], satt[:, 2 * E + 2:2 * E + 3], -1.0, None,
                                            ALU.mult).then_inc(mlp_dve, 1)
                    dve.wait_ge(mlp_act, 3)
                    nc.vector.reciprocal(satt[:, 2 * E + 3:2 * E + 4], satt[:, 2 * E + 1:2 * E + 2]).then_inc(mlp_dve, 1)
                    dve.wait_ge(mlp_dve, 3)
                    nc.vector.tensor_scalar(satt[:, E:2 * E], satt[:, 0:E], satt[:, 2 * E + 3:2 * E + 4], None,
                                            ALU.mult).then_inc(mlp_dve, 1)
                    dve.wait_ge(mlp_mm, 4)
                    nc.vector.tensor_copy(att_t[:], bank[3][0:E, 0:B]).then_inc(att_ready, 1)
                dve.wait_ge(agg_mm, blk + 1)
                for h in range(2):
                    nc.vector.tensor_copy(agg[:, h * 32:(h + 1) * 32], bank[4 + h][:].rearrange("p (o b) -> p o b", b=BB)).then_inc(agg_ready, 1)
                bias_ps = bank[6][:, 0:BB].rearrange("p (q c) -> p q c", c=2)
                for c in range(2):
                    nc.vector.tensor_copy(aggb[64 * c:64 * c + 64, :], bias_ps[64 * c:64 * c + 64, :, c]).then_inc(agg_ready, 1)
                dve.wait_ge(agg_ready, 4 * (blk + 1))
                dve.wait_ge(bdg_zero, blk + 1)

                for i in rounds(dve, PAIRS // 2):
                    for k in range(2):
                        wait(dve, z_mm, i * 2 + (PAIRS * blk + k - 1))
                        for c in range(2):
                            src = agg[64 * c:64 * c + 64, :, bass.ds(i * 4 + (2 * k + c), 1)].rearrange("p o b -> p (o b)")
                            nc.vector.tensor_copy(bdg[64 * c:64 * c + 64, k, 64 * c:64 * c + 64], src).then_inc(bdg_ready, 1)
                        dve.wait_ge(z_tr, i * 2 + (PAIRS * blk + k + 1))
                        wait(dve, gate_mm, i * 2 + (PAIRS * blk + k - 1))
                        for h in range(2):
                            nc.vector.tensor_copy(zt[:, k, h * 512:(h + 1) * 512], bank[4 + h][:]).then_inc(zt_ready, 1)
                        dve.wait_ge(gate_mm, i * 2 + (PAIRS * blk + k + 1))
                        nc.vector.tensor_copy(logits[:, bass.ds(i * 2 + (PAIRS * blk + k), 1)],
                                              bank[6 + k][:, 0:E].rearrange("p (a e) -> p a e", a=1)).then_inc(logit_ready, 1)

            step = [0]

            def link(ins):
                step[0] += 1
                ins.then_inc(route_dve, 1)
                dve.wait_ge(route_dve, step[0])

            dve.wait_ge(logit_ready, TILES)
            for k in range(2):
                dve.wait_ge(z_stored[k], 16 * TILES // 2)
            dve.wait_ge(x_stored, 32)
            dve.wait_ge(iotas, 5)
            for t in range(TILES):
                ins = nc.vector.max(top[:, t], logits[:, t])
            link(ins)
            for t in range(TILES):
                ins = nc.vector.max_index(topi[:, t], top[:, t], logits[:, t])
            link(ins)
            nc.vector.tensor_copy(iota_sf[:], iota_s[:])
            nc.vector.tensor_copy(iota_ef[:], iota_e[:])
            link(nc.vector.tensor_copy(eid[:], topi[:, :, 0]))
            link(nc.vector.tensor_tensor(oh[:], eid[:].rearrange("p (t o) -> p t o", o=1).broadcast_to([P, TILES, E]),
                                         iota_ef[:].rearrange("p (o e) -> p o e", o=1).broadcast_to([P, TILES, E]), ALU.is_equal))
            link(nc.vector.memset(run[:, 0], 0.0))
            dve.wait_ge(route_mm, 1)
            total = bank[1][:, 0:P].rearrange("p (t e) -> p t e", e=E)
            for t in range(TILES):
                link(nc.vector.tensor_tensor(run[:, t + 1], run[:, t], total[:, t], ALU.add))
            link(nc.vector.tensor_scalar(cnt[:], run[:, TILES], float(ST - 1), None, ALU.add))
            link(nc.vector.tensor_single_scalar(cnt2[:], cnt[:], ST.bit_length() - 1, ALU.arith_shift_right))
            link(nc.vector.tensor_copy(ntl[:], cnt2[:]))
            link(nc.vector.memset(end[:, 0:1], 0.0))
            for e in range(E):
                link(nc.vector.tensor_tensor(end[:, e + 1:e + 2], end[:, e:e + 1], ntl[:, e:e + 1], ALU.add))
            link(nc.vector.tensor_tensor(place[:], bank[0][:, 0:P].rearrange("p (t e) -> p t e", e=E), run[:, 0:TILES], ALU.add))
            link(nc.vector.scalar_tensor_tensor(out=place[:], in0=end[:, 0:E].rearrange("p (o e) -> p o e", o=1).broadcast_to([P, TILES, E]),
                                                scalar=float(ST), in1=place[:], op0=ALU.mult, op1=ALU.add))
            link(nc.vector.tensor_tensor(place[:], place[:], oh[:], ALU.mult))
            link(nc.vector.reduce_sum(slotf[:], place[:], AX.X))
            link(nc.vector.tensor_copy(sloti[:, 0], slotf[:]))
            nc.vector.tensor_single_scalar(sloti[:, 1], sloti[:, 0], P - 1, ALU.bitwise_and)
            link(nc.vector.tensor_single_scalar(sloti[:, 2], sloti[:, 0], P.bit_length() - 1, ALU.arith_shift_right))
            link(nc.vector.tensor_copy(slotp[:], sloti[:, 1:3]))
            nc.vector.scalar_tensor_tensor(out=sloti[:, 3], in0=slotp[:, 0], scalar=float(SC), in1=slotp[:, 1], op0=ALU.mult,
                                           op1=ALU.add).then_inc(slots_ready, 1)
            link(nc.vector.tensor_tensor(past[:], end[:, 1:E + 1].rearrange("p (o e) -> p o e", o=1).broadcast_to([P, 16, E]),
                                         iota_sf[:].rearrange("p (s o) -> p s o", o=1).broadcast_to([P, 16, E]), ALU.is_le))
            link(nc.vector.reduce_sum(etf[:], past[:], AX.X))
            nc.vector.tensor_scalar(eti[:], etf[:], float(E - 1), None, ALU.min).then_inc(tiles_ready, 1)

            def chunk_low(i, par, kt):
                dve.wait_ge(whr_ready, i * 16 + (8 * par + kt + 1))
                nc.vector.tensor_tensor(wlr[:, kt % 4], wraw[:, kt], whr[:, kt % 4], ALU.subtract).then_inc(wlr_ready, 1)

            def z_low(i, par):
                for b in range(4):
                    dve.wait_ge(zth_ready, i * 8 + (4 * par + b + 1))
                    nc.vector.tensor_tensor(ztl[:, par, 2 * b:2 * b + 2], bank[4 * par + b][:].rearrange("p (k s) -> p k s", k=2),
                                            zth[:, par, 2 * b:2 * b + 2], ALU.subtract).then_inc(ztl_ready, 1)

            def add_bias(i, par):
                dve.wait_ge(eb_in[par], i * 16 + 16)
                dve.wait_ge(zx_in[par], i * 32 + 32)
                a = zx[:, par, :, L:2 * L]
                nc.vector.tensor_tensor(a, a, ebs[:, par:par + 1].broadcast_to([P, 2, L]), ALU.add).then_inc(xb_ready, 1)

            def add_rows(i, par):
                wait(dve, chunk_mm, i * 16 + (8 * par + 8))
                dve.wait_ge(xb_ready, i * 2 + (par + 1))
                for b in range(4):
                    a = zx[:, par, b // 2, L + (b % 2) * 512:L + (b % 2 + 1) * 512]
                    nc.vector.tensor_tensor(a, a, bank[4 * par + b][:], ALU.add).then_inc(y_ready, 1)

            def expert(i, par, nxt, last):
                for kt in range(KT):
                    chunk_low(i, par, kt)
                    if kt == 0 and last:
                        add_rows(*last)
                    if kt == 3:
                        add_bias(i, par)
                    if kt == 5 and nxt:
                        z_low(*nxt)

            z_low(0, 0)
            for i in rounds(dve, NS // 2):
                expert(i, 0, (i, 1), (i - 1, 1) if not isinstance(i, int) else None)
                expert(i, 1, (i + 1, 0), (i, 0))
            expert(NS // 2, 0, None, (NS // 2 - 1, 1))
            add_rows(NS // 2, 0)

        @block.tensor
        def _(pe):
            mm = nc.tensor.matmul

            def three(ps, ah, al, bh, bl, first, last):
                mm(ps, ah, bh, start=first, stop=False)
                mm(ps, ah, bl, start=False, stop=False)
                return mm(ps, al, bh, start=False, stop=last)

            pe.wait_ge(ident_ready, 2)
            pe.wait_ge(ones_ready, 1)
            for blk in range(BLKS):
                pe.wait_ge(cprod_ready, blk + 1)
                for h in range(2):
                    mm(bank[h][:], ones[:], cprod[:, h * 8:(h + 1) * 8], start=True, stop=False)
                    ins = mm(bank[h][:], ones[0:1, :], cbias[:].rearrange("p (b o) -> p b o", b=1).broadcast_to([1, 8, CH]),
                             start=False, stop=True)
                ins.then_inc(ctx_mm, 1)
                for i in rounds(pe, BB // 4):
                    for k in range(4):
                        if k % 2 == 0:
                            pe.wait_ge(xcv_in[k // 2], i * 16 + (16 * PAIRS // 2 * blk + 16))
                        wait(pe, x32_ready, i * 4 + (BB * blk + k - 3))
                        for g in range(GROUPS):
                            for d in range(2):
                                ins = mm(bank[4 + k][:, g * P:(g + 1) * P], xcv[:, k // 2, k % 2, g, d:d + P], tz[:, d, g],
                                         start=d == 0, stop=d == 1)
                        ins.then_inc(conv_mm, 1)

                def lora_product(i, n):
                    if blk:
                        return
                    s = n % 2
                    if n % 4 < 2:
                        pe.wait_ge(lora_in[s], i * 64 + 32 * (n // 4 + 1))
                    wait(pe, w_ready, i * 8 + n)
                    for h in range(2):
                        if n % 4 < 2:
                            for q in range(4):
                                ins = mm(bank[2 + h][:, q * P:(q + 1) * P], lora[0:R, (4 * h + q) * P:(4 * h + q + 1) * P],
                                         lora_t[0:R, s], start=True, stop=True)
                        else:
                            ins = mm(bank[2 + h], lora_t[32:32 + R, s], lora[32:32 + R, h * 512:(h + 1) * 512],
                                     start=True, stop=True)
                    ins.then_inc(ab_mm, 1)

                def up(i, w, between=None):
                    half, par = w % 2, (w // 2) % 2
                    pe.wait_ge(wl_ready, i * 8 + (JOBS * blk + 4 * (w // 2) + 2))
                    wait(pe, hl_ready, i * 4 + (NU * blk + w))
                    t0 = half * HALF
                    for s in range(2):
                        for kt in range(KT):
                            c = slice(kt * P, (kt + 1) * P)
                            ins = three(bank[s], wuh[:, 2 * par + s, c], wul[:, 2 * par + s, c], x1h[:, kt, t0:t0 + HALF],
                                        x1l[:, kt, t0:t0 + HALF], kt == 0, kt == KT - 1)
                        if s == 0 and between:
                            lora_product(*between)
                    ins.then_inc(up_mm, 1)

                def down(i, u, between=None):
                    par, hp = (u // 2) % 2, u % 2
                    pe.wait_ge(wl_ready, i * 8 + (JOBS * blk + 4 * (u // 2) + 4))
                    pe.wait_ge(hl_ready, i * 4 + (NU * blk + u + 1))
                    for j in range(4):
                        wait(pe, acc_added, i * 16 + (4 * (NU * blk + u) + j - 1))
                        c = slice(j * P, (j + 1) * P)
                        for dh in range(2):
                            d = slice(dh * 512, (dh + 1) * 512)
                            for s in range(2):
                                ins = three(bank[4 + 2 * (j % 2) + dh], hh[:, 2 * hp + s, c], hl[:, 2 * hp + s, c],
                                            wdh[:, 2 * par + s, d], wdl[:, 2 * par + s, d], s == 0, s == 1)
                        ins.then_inc(dn_mm, 1)
                        if j == 1 and between:
                            lora_product(*between)

                pe.wait_ge(x1l_ready, BB * (blk + 1))
                pe.wait_ge(ffn_const, 48 * (blk + 1))
                for n in range(3):
                    lora_product(0, n)
                up(0, 0, (0, 3))
                lora_product(0, 4)
                for i in rounds(pe, ROUNDS, last=True):
                    for k in range(4):
                        jobs = stage_jobs(i, k)
                        up(i, k + 1, (i, 5 + 2 * k))
                        down(i, k, jobs[0] if jobs else None)
                up(ROUNDS, 1)
                down(ROUNDS, 0)
                down(ROUNDS, 1)

                pe.wait_ge(acc_added, 4 * NU * (blk + 1))
                pe.wait_ge(dyn_const, 16 * (CONSTS_DYN + 4 * blk))
                if blk == 0:
                    ins = mm(bank[0][:, 0:B], w0s[:], ct2[:], start=True, stop=True)
                    ins.then_inc(mlp_mm, 1)
                    pe.wait_ge(mlp_act, 1)
                    mm(bank[1][:, 0:B], w1s[:], hid1[:], start=True, stop=True).then_inc(mlp_mm, 1)
                    pe.wait_ge(mlp_act, 2)
                    mm(bank[2][0:B, 0:E], hid2[:], w2s[:], start=True, stop=False)
                    mm(bank[2][0:B, 0:E], ones[0:1, 0:B], b2s[:], start=False, stop=True).then_inc(mlp_mm, 1)
                    pe.wait_ge(mlp_dve, 4)
                    nc.tensor.transpose(bank[3][0:E, 0:B], satt[:, E:2 * E], ident[0:B, 0:B]).then_inc(mlp_mm, 1)
                    pe.wait_ge(att_ready, 1)
                att = att_t[:, BB * blk:BB * (blk + 1)]
                for o in range(CH):
                    mm(bank[4 + o // 32][:, (o % 32) * BB:(o % 32 + 1) * BB], kerns[:, o], att, start=True, stop=True)
                mm(bank[6][:, 0:BB], kernb[:], att, start=True, stop=True).then_inc(agg_mm, 1)

                for i in rounds(pe, PAIRS // 2):
                    for k in range(2):
                        pe.wait_ge(bdg_ready, i * 4 + (2 * PAIRS * blk + 2 * k + 2))
                        wait(pe, z_ready, i * 4 + (2 * PAIRS * blk + 2 * k - 2))
                        for h in range(2):
                            rows = acc[:, bass.ds(i * 2 + k, 1), h * 512:(h + 1) * 512].rearrange("p a l -> p (a l)")
                            ins = mm(bank[2 * k + h][:], bdg[:, k], rows, start=True, stop=True)
                        ins.then_inc(z_mm, 1)
                        pe.wait_ge(z_ready, i * 4 + (2 * PAIRS * blk + 2 * k + 2))
                        wait(pe, zt_ready, i * 4 + (2 * PAIRS * blk + 2 * k))
                        for kt in range(KT):
                            ins = nc.tensor.transpose(bank[4 + kt // 4][:, (kt % 4) * P:(kt % 4 + 1) * P],
                                                      z32[:, k, kt * P:(kt + 1) * P], ident[:])
                        ins.then_inc(z_tr, 1)
                        pe.wait_ge(zt_ready, i * 4 + (2 * PAIRS * blk + 2 * k + 2))
                        wait(pe, logit_ready, i * 2 + (PAIRS * blk + k - 1))
                        mm(bank[6 + k][:, 0:E], ones[0:1, :], gbs[:], start=True, stop=False)
                        for kt in range(KT):
                            ins = mm(bank[6 + k][:, 0:E], zt[:, k, kt * P:(kt + 1) * P], gts[:, kt], start=False, stop=kt == KT - 1)
                        ins.then_inc(gate_mm, 1)

            pe.wait_ge(route_dve, ONEHOT)
            pe.wait_ge(iotas, 5)
            mm(bank[0][:, 0:P], tri[:], oh[:].rearrange("p t e -> p (t e)"), start=True, stop=True)
            mm(bank[1][:, 0:P], ones[:], oh[:].rearrange("p t e -> p (t e)"), start=True, stop=True).then_inc(route_mm, 1)
            pe.wait_ge(slots_ready, 1)

            def rows_transposed(i, par):
                pe.wait_ge(zx_in[par], i * 32 + 32)
                wait(pe, y_ready, i * 8 + (4 * par - 4))
                for b in range(4):
                    for q in range(4):
                        kt, h = 2 * b + q // 2, q % 2
                        ins = nc.tensor.transpose(bank[4 * par + b][:, q * P:(q + 1) * P], zx[:, par, h, kt * P:(kt + 1) * P], ident[:])
                    ins.then_inc(tr_mm, 1)

            def chunk(i, par, kt):
                pe.wait_ge(wlr_ready, i * 16 + (8 * par + kt + 1))
                if kt == 0:
                    pe.wait_ge(ztl_ready, i * 8 + (4 * par + 4))
                for b in range(4):
                    s, d = slice((b // 2) * P, (b // 2 + 1) * P), slice((b % 2) * 512, (b % 2 + 1) * 512)
                    ins = three(bank[4 * par + b][:], zth[:, par, kt, s], ztl[:, par, kt, s], whr[:, kt % 4, d], wlr[:, kt % 4, d],
                                kt == 0, kt == KT - 1)
                ins.then_inc(chunk_mm, 1)

            def expert(i, par, nxt):
                for kt in range(KT):
                    chunk(i, par, kt)
                    if kt == 3 and nxt:
                        rows_transposed(*nxt)

            rows_transposed(0, 0)
            for i in rounds(pe, NS // 2):
                expert(i, 0, (i, 1))
                expert(i, 1, (i + 1, 0))
            expert(NS // 2, 0, None)


def layouts(x, cond_128, fside_S_0, L0_cond_weight, L0_cond_c_weight, L0_ffn_w_up_codes, L0_ffn_w_up_absmax,
            L0_ffn_b_up, L0_ffn_w_up_lora_a, L0_ffn_w_up_lora_b, L0_ffn_w_down_codes, L0_ffn_w_down_absmax, L0_ffn_b_down,
            L0_ffn_w_down_lora_a, L0_ffn_w_down_lora_b, L1_cond_W0, L1_cond_b0, L1_cond_W1, L1_cond_b1, L1_cond_W2,
            L1_cond_b2, L1_cond_weight, L1_cond_bias_k, L1_ffn_gate_w, L1_ffn_gate_b, L1_ffn_expert_w, L1_ffn_expert_b):
    def padded(a, axis, size):
        room = [(0, 0)] * a.ndim
        room[axis] = (0, size - a.shape[axis])
        return np.pad(a, room)

    half = TAPS // 2
    xp = np.pad(x, ((0, 0), (0, 0), (half, J * MB - L - half)))
    x_conv = xp.reshape(B, GROUPS, GC, MB, J).transpose(2, 4, 0, 1, 3).reshape(P, B, GROUPS, MB)
    w = L0_cond_weight.reshape(GROUPS, GC, GC, TAPS)
    toep = np.zeros((GC, J, 2, GROUPS, J, GC), w.dtype)
    for d in range(2):
        for jp in range(J):
            for j in range(J):
                tap = J * d + jp - j
                if 0 <= tap < TAPS:
                    toep[:, jp, d, :, j, :] = w[:, :, :, tap].transpose(2, 0, 1)
    cu = padded(L0_ffn_w_up_codes.reshape(HID, P, J), 0, NT * P).reshape(NT, P, P, J).transpose(0, 2, 3, 1)
    cd = padded(L0_ffn_w_down_codes.reshape(L, HID).T, 0, NT * P).reshape(NT, P, L)
    au = padded(L0_ffn_w_up_absmax.reshape(HID, 16), 0, NT * P).reshape(NT, P, 16).transpose(0, 2, 1)
    ad = padded(L0_ffn_w_down_absmax.reshape(L, HID // 64).T, 0, 2 * NT).reshape(NT, 2, L)
    kern = L1_cond_weight[..., 0]
    return dict(
        x_nat=x.reshape(N, L), x_conv=x_conv, toep=toep.reshape(P, 2, GROUPS, P), cond_t=cond_128.T,
        ctx_w_t=L0_cond_c_weight.T, chan_bias=fside_S_0.reshape(1, CH), codes_up=cu.reshape(NT, P, L), codes_dn=cd,
        am_up=au, am_dn=ad, bias_up=padded(L0_ffn_b_up, 0, NT * P).reshape(NT, P).T, bias_dn=L0_ffn_b_down.reshape(1, L),
        lora_up_at=L0_ffn_w_up_lora_a.reshape(P, J, R).transpose(2, 1, 0).reshape(R, L),
        lora_up_b=padded(L0_ffn_w_up_lora_b, 1, NT * P).reshape(R, NT, P).transpose(1, 0, 2),
        lora_dn_at=padded(L0_ffn_w_down_lora_a, 0, NT * P).reshape(NT, P, R).transpose(0, 2, 1),
        lora_dn_b=L0_ffn_w_down_lora_b, w0=L1_cond_W0, b0=L1_cond_b0.reshape(P, 1), w1=L1_cond_W1,
        b1=L1_cond_b1.reshape(P, 1), w2=L1_cond_W2, b2=L1_cond_b2.reshape(1, E),
        kern=np.concatenate([kern, kern], 2), kern_b=np.concatenate([L1_cond_bias_k] * 2, 1),
        gate_t=L1_ffn_gate_w.T.reshape(KT, P, E).transpose(1, 0, 2), gate_b=L1_ffn_gate_b.reshape(1, E),
        exp_w=L1_ffn_expert_w.transpose(0, 2, 1).reshape(E, KT, P, L).transpose(0, 2, 1, 3), exp_b=L1_ffn_expert_b)


def kernel(**inputs):
    import concourse.bacc as bacc
    from concourse.bass_utils import run_bass_kernel_spmd

    arrays = {name: np.ascontiguousarray(a) for name, a in layouts(**{k: np.asarray(a) for k, a in inputs.items()}).items()}
    nc = bacc.Bacc("TRN2", target_bir_lowering=False, num_devices=1)
    args = {name: nc.dram_tensor(name, a.shape, mybir.dt.from_np(a.dtype), kind="ExternalInput").ap()
            for name, a in arrays.items()}
    out = nc.dram_tensor("out", (N, L), F32, kind="ExternalOutput").ap()
    program(nc, out=out, **args)
    result = run_bass_kernel_spmd(nc, [arrays], core_ids=[0])
    return result.results[0]["out"].reshape(B, CH, L)
```

```python
from contextlib import ExitStack

import concourse.bass as bass
import numpy as np
from concourse import mybir

F32 = mybir.dt.float32
F32R = mybir.dt.float32r
I32 = mybir.dt.int32
U32 = mybir.dt.uint32
ALU = mybir.AluOpType
ACT = mybir.ActivationFunctionType
AX = mybir.AxisListType

P = 128
B, CH, L = 32, 64, 1024
GROUPS, TAPS = 4, 9
GC = CH // GROUPS
J = P // GC
MB = L // J + 1
N = B * CH
BLKS = 2
NB = N // BLKS
BB = B // BLKS
HID = 2752
NT = -(-HID // P)
NG = NT // 2
HALF = 512
ROUNDS = NG // 2
AHEAD = 6
NU = 2 * NG
JOBS = 4 * NG
KT = L // P
R = 16
E = 8
PAIRS = BB // 2
TILES = N // P
ST = 256
NS = (N + E * (ST - 1)) // ST
SC = NS * ST // P
ONEHOT = 4

NF4 = np.array([-1.0, -0.6961928009986877, -0.5250730514526367, -0.39491748809814453, -0.28444138169288635,
                -0.18477343022823334, -0.09105003625154495, 0.0, 0.07958029955625534, 0.16093020141124725,
                0.24611230194568634, 0.33791524171829224, 0.44070982933044434, 0.5626170039176941,
                0.7229568362236023, 1.0], np.float32)


def nf4_terms():
    f, terms = NF4.astype(np.float64), []
    for sign, near in ((1, 8), (-1, 7)):
        slope = base = 0.0
        side = []
        for n in range(4):
            c = near + 2 * sign * n
            new_slope = sign * (f[c + sign] - f[c])
            new_base = f[c] - new_slope * c
            side.append((sign, float(sign * (new_slope - slope)), float((base - new_base) / (new_slope - slope))))
            slope, base = new_slope, new_base
        terms += side[::-1]
    return terms


def wait(eng, sem, value):
    if isinstance(value, int) and value <= 0:
        return
    eng.wait_ge(sem, value)


def rounds(eng, n, last=False):
    yield 0
    with eng.Fori(1, n - last) as i:
        yield i
    if last:
        yield n - 1


def stage_jobs(i, k):
    if isinstance(i, int) and i == ROUNDS - 1 and k == 3:
        return ()
    return (i, 6 + 2 * k), (i, 7 + 2 * k)


def program(nc, x_nat, x_conv, toep, cond_t, ctx_w_t, chan_bias, codes_up, codes_dn, am_up, am_dn, bias_up, bias_dn,
            lora_up_at, lora_up_b, lora_dn_at, lora_dn_b, w0, b0, w1, b1, w2, b2, kern, kern_b, gate_t, gate_b,
            exp_w, exp_b, out):
    TERMS = nf4_terms()
    NHEAD = 3
    CHAIN = TERMS[NHEAD:]
    NCH = len(CHAIN)
    ctx = ExitStack()
    with ctx:
        def sem(name):
            return ctx.enter_context(nc.semaphore(name))

        def sb(stack, name, shape, dt=F32):
            return stack.enter_context(nc.sbuf_tensor(name, shape, dt))

        bd_dram = nc.dram_tensor("pair_kernels", (TILES, P, P), F32, kind="Internal").ap()
        w_dram = nc.dram_tensor("w_dequantised", (JOBS, P, L), F32, kind="Internal").ap()
        z_dram = nc.dram_tensor("z_rows", (N, L), F32, kind="Internal").ap()
        x_dram = nc.dram_tensor("x_rows", (N, L), F32, kind="Internal").ap()
        slot_dram = nc.dram_tensor("slot_token", (P * SC, 1), I32, kind="Internal").ap()

        ident = sb(ctx, "ident", [P, P])
        ones = sb(ctx, "ones", [P, P])
        att_t = sb(ctx, "att_t", [E, B])
        logits = sb(ctx, "logits", [P, TILES, E])
        aggb = sb(ctx, "aggb", [P, TILES])
        gts = sb(ctx, "gts", [P, KT, E])
        gbs = sb(ctx, "gbs", [1, E])

        mlp = ExitStack()
        kerns = sb(mlp, "kerns", [E, CH, P])
        kernb = sb(mlp, "kernb", [E, P])
        ct2 = sb(mlp, "ct2", [P, B])
        w0s = sb(mlp, "w0s", [P, P])
        w1s = sb(mlp, "w1s", [P, P])
        w2s = sb(mlp, "w2s", [P, E])
        b0s = sb(mlp, "b0s", [P, 1])
        b1s = sb(mlp, "b1s", [P, 1])
        b2s = sb(mlp, "b2s", [1, E])
        hid1 = sb(mlp, "hid1", [P, B])
        hid2 = sb(mlp, "hid2", [P, B])
        satt = sb(mlp, "satt", [B, 3 * E])
        bds = sb(mlp, "bds", [P, TILES, P])
        mlp.close()

        late = ExitStack()
        acc = sb(late, "acc", [P, PAIRS, L])
        x1h = sb(late, "x1h", [P, KT, NB], F32R)
        x1l = sb(late, "x1l", [P, KT, NB], F32R)
        am = sb(late, "am", [P, L])
        lora = sb(late, "lora", [48, L])
        lora_t = sb(late, "lora_t", [48, 2, P])
        bup = sb(late, "bup", [P, NT])
        low_parts = ExitStack()
        wul = sb(low_parts, "wul", [P, 4, L], F32R)
        wdl = sb(low_parts, "wdl", [P, 4, L], F32R)
        low_parts.close()
        wu = sb(late, "wu", [P, 4, L])
        wd = sb(late, "wd", [P, 4, L])
        wuh = sb(late, "wuh", [P, 4, L], F32R)

        conv = ExitStack()
        tz = sb(conv, "tz", [P, 2, GROUPS, P])
        cprod = sb(conv, "cprod", [P, BB, CH])
        ctxb = sb(conv, "ctxb", [P, NB])
        bdn = sb(conv, "bdn", [P, L])
        x32 = sb(conv, "x32", [P, 2, KT, CH])
        xcv = sb(conv, "xcv", [P, 2, 2, GROUPS, MB])
        ct = sb(conv, "ct", [P, B])
        cwt = sb(conv, "cwt", [P, CH])
        cbias = sb(conv, "cbias", [1, CH])
        conv.close()
        wdh = sb(late, "wdh", [P, 4, L], F32R)
        hh = sb(late, "hh", [P, 4, HALF], F32R)
        hl = sb(late, "hl", [P, 4, HALF], F32R)

        dyn = ExitStack()
        z32 = sb(dyn, "z32", [P, 2, L])
        zt = sb(dyn, "zt", [P, L])
        bdg = sb(dyn, "bdg", [P, 2, P])
        dyn.close()
        term = sb(late, "term", [P, 2, L])
        hterm = sb(late, "hterm", [P, L])
        codes = sb(late, "codes", [P, 2, L], I32)
        late.close()

        moe = ExitStack()
        whr = sb(moe, "whr", [P, 4, L], F32R)
        wlr = sb(moe, "wlr", [P, 4, L], F32R)
        zth = sb(moe, "zth", [P, 2, KT, ST], F32R)
        ztl = sb(moe, "ztl", [P, 2, KT, ST], F32R)
        wraw = sb(moe, "wraw", [P, KT, L])
        zg = sb(moe, "zg", [P, 2, 2, L])
        xg = sb(moe, "xg", [P, 2, 2, L])
        ebs = sb(moe, "ebs", [P, 2, L])
        tri = sb(moe, "tri", [P, P])
        top = sb(moe, "top", [P, TILES, E])
        topi = sb(moe, "topi", [P, TILES, E], U32)
        eid = sb(moe, "eid", [P, TILES])
        iota_e = sb(moe, "iota_e", [P, E], I32)
        iota_ef = sb(moe, "iota_ef", [P, E])
        iota_s = sb(moe, "iota_s", [P, 16], I32)
        iota_sf = sb(moe, "iota_sf", [P, 16])
        oh = sb(moe, "oh", [P, TILES, E])
        run = sb(moe, "run", [P, TILES + 1, E])
        cnt = sb(moe, "cnt", [P, E], I32)
        cnt2 = sb(moe, "cnt2", [P, E], I32)
        ntl = sb(moe, "ntl", [P, E])
        end = sb(moe, "end", [P, E + 1])
        place = sb(moe, "place", [P, TILES, E])
        slotf = sb(moe, "slotf", [P, TILES])
        sloti = sb(moe, "sloti", [P, 4, TILES], I32)
        slotp = sb(moe, "slotp", [P, 2, TILES])
        tokid = sb(moe, "tokid", [P, TILES], I32)
        nobody = sb(moe, "nobody", [P, SC], I32)
        table = sb(moe, "table", [P, SC], I32)
        past = sb(moe, "past", [P, 16, E])
        etf = sb(moe, "etf", [P, 16])
        eti = sb(moe, "eti", [P, 16], I32)
        zidx = sb(moe, "zidx", [P, 4], I32)
        xidx = sb(moe, "xidx", [P, 4], I32)
        moe.close()

        pair = [ctx.enter_context(nc.psum_tensor(f"pair{i}", [P, 1024], F32)) for i in range(4)]
        bank = [pair[i // 2][:, i % 2 * 512:(i % 2 + 1) * 512] for i in range(8)]

        ident_ready, ones_ready = sem("ident_ready"), sem("ones_ready")
        conv_const = sem("conv_const")
        xcv_in = [sem(f"xcv_in{i}") for i in range(2)]
        acc_in, bdn_in = sem("acc_in"), sem("bdn_in")
        cprod_ready, ctx_mm, ctxb_ready = sem("cprod_ready"), sem("ctx_mm"), sem("ctxb_ready")
        conv_mm, x32_ready, x1h_ready, x1l_ready = sem("conv_mm"), sem("x32_ready"), sem("x1h_ready"), sem("x1l_ready")
        acc_bias = sem("acc_bias")
        ffn_const = sem("ffn_const")
        codes_in = [sem(f"codes_in{i}") for i in range(2)]
        am_in = sem("am_in")
        lora_in = [sem(f"lora_in{i}") for i in range(2)]
        head_terms, head_added = sem("head_terms"), sem("head_added")
        term_ready, term_added, scaled, ab_mm, w_ready = (sem(n) for n in (
            "term_ready", "term_added", "scaled", "ab_mm", "w_ready"))
        w_stored = [sem(f"w_stored{i}") for i in range(2)]
        w_in = [sem(f"w_in{i}") for i in range(8)]
        wh_ready, wl_ready = sem("wh_ready"), sem("wl_ready")
        up_mm, relu_done, hh_ready, hl_ready = sem("up_mm"), sem("relu_done"), sem("hh_ready"), sem("hl_ready")
        dn_mm, acc_added = sem("dn_mm"), sem("acc_added")
        mlp_const, mlp_mm, mlp_act, mlp_dve, att_ready = (sem(n) for n in (
            "mlp_const", "mlp_mm", "mlp_act", "mlp_dve", "att_ready"))
        agg_mm, agg_ready, bds_zero, bds_stored = sem("agg_mm"), sem("agg_ready"), sem("bds_zero"), sem("bds_stored")
        aggb_ready = sem("aggb_ready")
        bdg_in = [sem(f"bdg_in{i}") for i in range(2)]
        z_mm, z_ready, z_tr, zt_ready, gate_mm, logit_ready = (sem(n) for n in (
            "z_mm", "z_ready", "z_tr", "zt_ready", "gate_mm", "logit_ready"))
        z_stored = [sem(f"z_stored{i}") for i in range(2)]
        x_stored = sem("x_stored")
        iotas, nobody_ready, table_clear, table_set, table_in = (sem(n) for n in (
            "iotas", "nobody_ready", "table_clear", "table_set", "table_in"))
        route_dve, route_mm, slots_ready, tiles_ready = (sem(n) for n in (
            "route_dve", "route_mm", "slots_ready", "tiles_ready"))
        rows_zero, zidx_ready, xidx_ready = sem("rows_zero"), sem("zidx_ready"), sem("xidx_ready")
        zg_in = [sem(f"zg_in{i}") for i in range(2)]
        xg_in = [sem(f"xg_in{i}") for i in range(2)]
        wraw_in = [sem(f"wraw_in{i}") for i in range(KT)]
        eb_in = [sem(f"eb_in{i}") for i in range(2)]
        whr_ready, wlr_ready, chunk_mm = sem("whr_ready"), sem("wlr_ready"), sem("chunk_mm")
        tr_mm, zth_ready, ztl_ready = sem("tr_mm"), sem("zth_ready"), sem("ztl_ready")
        xb_ready, y_ready = sem("xb_ready"), sem("y_ready")
        out_done = [sem(f"out_done{i}") for i in range(2)]

        act_passed, pool_passed = sem("act_passed"), sem("pool_passed")

        def slot(n):
            return 2 * (n // 4 % 2) + n % 2

        def whole(n):
            return (wu if n % 4 < 2 else wd)[:, slot(n)]

        def high_part(n):
            return (wuh if n % 4 < 2 else wdh)[:, slot(n)]

        def low_part(n):
            return (wul if n % 4 < 2 else wdl)[:, slot(n)]

        def wait_place(eng, i, n, blk):
            before = NU * blk + 2 * (n // 4) - 2
            if n % 4 < 2:
                wait(eng, up_mm, i * 4 + before)
            else:
                wait(eng, dn_mm, i * 16 + 4 * before)

        block = ctx.enter_context(nc.Block())

        MLP_CONSTS = 11
        STEPS = BLKS + 1

        @block.sync
        def _(sp):
            for dst, src in ((ct2[:], cond_t), (w0s[:], w0), (b0s[:], b0), (w1s[:], w1), (b1s[:], b1), (w2s[:], w2),
                             (b2s[:], b2), (kerns[:], kern), (kernb[:], kern_b), (gts[:], gate_t), (gbs[:], gate_b)):
                sp.dma_start(dst, src).then_inc(mlp_const, 16)
            for blk in range(STEPS):
                def load_scales(i, n):
                    t = i * 4 + (2 * (n // 4) + n % 2)
                    wait(sp, scaled, i * 8 + n)
                    if n % 4 < 2:
                        sp.dma_start(am[:, 0:P].rearrange("p (o n) -> p o n", o=1), am_up[bass.ds(t, 1)].rearrange(
                            "a k (o n) -> (a k) o n", o=1).broadcast_to([16, 8, P])).then_inc(am_in, 16)
                    else:
                        sp.dma_start(am[:], am_dn[bass.ds(t, 1)].rearrange("a k (o n) -> (a k) o n", o=1)
                                     .broadcast_to([2, 64, L])).then_inc(am_in, 16)

                def load(i, n):
                    s, t = n % 2, i * 4 + (2 * (n // 4) + n % 2)
                    if blk == 0:
                        wait(sp, term_ready, i * (8 * NCH) + NCH * (n - 1))
                        src = codes_up if n % 4 < 2 else codes_dn
                        sp.dma_start(codes[:, s], src[bass.ds(t, 1)].rearrange("a p n -> p (a n)")).then_inc(codes_in[s], 16)
                        if not isinstance(i, int) or i * 8 + n > 0:
                            load_scales(i, n - 1)
                        if n % 4 < 2:
                            wait(sp, ab_mm, i * 8 + (n - 1))
                            sp.dma_start(lora_t[0:R, s], lora_up_b[bass.ds(t, 1)].rearrange("a r n -> (a r) n")).then_inc(lora_in[s], 16)
                            sp.dma_start(lora_t[32:32 + R, s], lora_dn_at[bass.ds(t, 1)].rearrange("a r n -> (a r) n")).then_inc(lora_in[s], 16)
                    else:
                        wait_place(sp, i, n, blk)
                        sp.dma_start(whole(n), w_dram[bass.ds(i * 8 + n, 1)].rearrange("a p n -> p (a n)")).then_inc(w_in[n % 8], 16)

                def load_rows():
                    sp.dma_start(acc[:], x_nat[blk * NB:(blk + 1) * NB].rearrange("(t p) l -> p t l", p=P)).then_inc(acc_in, 16)

                if blk < BLKS:
                    wait(sp, dn_mm, 4 * NU * blk)
                    for dst, src in ((tz[:], toep), (ct[:], cond_t), (cwt[:], ctx_w_t), (cbias[:], chan_bias)):
                        sp.dma_start(dst, src).then_inc(conv_const, 16)
                    sp.dma_start(bdn[:], bias_dn[0:1, :].broadcast_to([P, L])).then_inc(bdn_in, 16)
                if blk == 0:
                    for dst, src in ((lora[0:R], lora_up_at), (lora[32:32 + R], lora_dn_b), (bup[:], bias_up)):
                        sp.dma_start(dst, src).then_inc(ffn_const, 16)
                else:
                    wait(sp, term_ready, JOBS * NCH)
                    wait(sp, bds_stored, 16)
                for i in rounds(sp, PAIRS // 2) if blk else range(PAIRS // 2):
                    for k in range(2):
                        if blk < BLKS:
                            wait(sp, conv_mm, i * 4 + (BB * blk + 2 * k - 2) if not isinstance(i, int) or i else 0)
                            sp.dma_start(xcv[:, k], x_conv[:, bass.ds(i * 4 + (BB * blk + 2 * k), 2)]).then_inc(xcv_in[k], 16)
                        if blk:
                            wait(sp, z_mm, i * 2 + (PAIRS * (blk - 1) + k - 1))
                            sp.dma_start(bdg[:, k], bd_dram[bass.ds(i * 2 + (PAIRS * (blk - 1) + k), 1)].rearrange(
                                "a p n -> p (a n)")).then_inc(bdg_in[k], 16)
                    if blk == 0:
                        if i == 0:
                            load(0, 0)
                            sp.wait_ge(agg_mm, 1)
                            load_rows()
                        load(0, i + 1)
                if blk == BLKS:
                    break
                if blk:
                    wait(sp, x_stored, 16 * blk)
                    wait(sp, z_mm, PAIRS * blk)
                    load_rows()
                for n in range(0 if blk else 5, AHEAD):
                    load(0, n)
                for i in rounds(sp, ROUNDS, last=True):
                    for k in range(4):
                        for job in stage_jobs(i, k):
                            load(*job)
                if blk == 0:
                    load_scales(0, JOBS - 1)

            wait(sp, logit_ready, TILES)
            for k in range(2):
                wait(sp, z_stored[k], 16 * TILES // 2)
            wait(sp, x_stored, 32)
            wait(sp, nobody_ready, 1)
            sp.dma_start(slot_dram.rearrange("(p c) o -> p (c o)", p=P), nobody[:]).then_inc(table_clear, 16)
            wait(sp, table_set, 16 * TILES)
            sp.dma_start(table[:], slot_dram.rearrange("(p c) o -> p (c o)", p=P)).then_inc(table_in, 16)
            wait(sp, tiles_ready, 1)

            def load_expert(i, par):
                e = sp.value_load(eti[0:1, bass.ds(i * 2 + par, 1)], min_val=0, max_val=E - 1)
                for kt in range(KT):
                    wait(sp, wlr_ready, i * 16 + (8 * par + kt - 7))
                    sp.dma_start(wraw[:, kt], exp_w[bass.ds(e, 1), :, kt].rearrange("a p n -> p (a n)")).then_inc(wraw_in[kt], 16)
                wait(sp, xb_ready, i * 2 + (par - 1))
                sp.dma_start(ebs[:, par], exp_b[bass.ds(e, 1)].broadcast_to([P, L])).then_inc(eb_in[par], 16)

            for i in rounds(sp, NS // 2):
                load_expert(i, 0)
                load_expert(i, 1)
            load_expert(NS // 2, 0)

        @block.gpsimd
        def _(pool):
            last_row = pool.to_reg(N - 1)
            nc.gpsimd.memset(ident[:], 0.0).then_inc(ident_ready, 1)
            nc.gpsimd.memset(ones[:], 1.0).then_inc(ones_ready, 1)
            pool.wait_ge(ident_ready, 1)
            nc.gpsimd.affine_select(out=ident[:], in_=ident[:], compare_op=ALU.not_equal, fill=1.0, base=0,
                                    pattern=[[-1, P]], channel_multiplier=1).then_inc(ident_ready, 1)

            def head(i, n, m):
                pool.wait_ge(head_terms, i * (8 * NHEAD) + (NHEAD * n + m + 1))
                if m > 1:
                    pool.wait_ge(head_added, i * 16 + (2 * n + m - 1))
                op = ALU.add if TERMS[m][0] > 0 else ALU.subtract
                nc.gpsimd.tensor_tensor(whole(n), whole(n), hterm[:], op).then_inc(head_added, 1)

            def low(i, n):
                pool.wait_ge(wh_ready, i * 8 + (n + 1))
                pool.wait_ge(w_stored[n % 2], i * 64 + 16 * (n // 2 + 1))
                nc.gpsimd.tensor_tensor(low_part(n), whole(n), high_part(n), ALU.subtract).then_inc(wl_ready, 1)

            def finish(i, n, more=True):
                if more:
                    head(i, n + 1, 1)
                if not isinstance(i, int) or i * 8 + n > 0:
                    low(i, n - 1)
                if more:
                    head(i, n + 1, 2)
                pool.wait_ge(term_added, i * (8 * NCH) + NCH * (n + 1))
                pool.wait_ge(am_in, i * 128 + 16 * (n + 1))
                if n % 4 < 2:
                    w = whole(n).rearrange("p (k n) -> p k n", n=P)
                    scale = am[:, 0:P].rearrange("p (o n) -> p o n", o=1).broadcast_to([P, KT, P])
                else:
                    w, scale = whole(n), am[:]
                nc.gpsimd.tensor_tensor(w, w, scale, ALU.mult).then_inc(scaled, 1)

            nc.gpsimd.memset(bds[:], 0.0).then_inc(bds_zero, 1)
            pool.wait_ge(agg_ready, 8)
            pool.dma_start(bd_dram.rearrange("q p n -> p q n"), bds[:]).then_inc(bds_stored, 16)

            def bias_rows(blk, tiles):
                pool.wait_ge(acc_in, 16 * (blk + 1))
                pool.wait_ge(bdn_in, 16 * (blk + 1))
                for t in tiles:
                    nc.gpsimd.tensor_tensor(acc[:, t], acc[:, t], bdn[:], ALU.add).then_inc(acc_bias, 1)

            for blk in range(STEPS):
                if blk:
                    wait(pool, acc_added, 4 * NU * blk)
                    pool.dma_start(x_dram[(blk - 1) * NB:blk * NB].rearrange("(t p) l -> p t l", p=P), acc[:]).then_inc(x_stored, 16)
                    for i in rounds(pool, PAIRS // 2):
                        for k in range(2):
                            wait(pool, z_ready, i * 2 + (PAIRS * (blk - 1) + k + 1))
                            pool.dma_start(z_dram[bass.ds(i * 2 * P + ((blk - 1) * NB + k * P), P)], z32[:, k]).then_inc(z_stored[k], 16)
                if blk == 0:
                    head(0, 0, 1)
                    head(0, 0, 2)
                    finish(0, 0)
                    for n in range(1, AHEAD):
                        finish(0, n)
                        if n < 5:
                            bias_rows(0, (2 * n - 2, 2 * n - 1))
                    for i in rounds(pool, ROUNDS, last=True):
                        for k in range(4):
                            for job in stage_jobs(i, k):
                                finish(*job, more=not isinstance(i, int) or i * 8 + job[1] < JOBS - 1)
                    low(0, JOBS - 1)
                elif blk < BLKS:
                    bias_rows(blk, range(PAIRS))

            wait(pool, logit_ready, TILES)
            for k in range(2):
                wait(pool, z_stored[k], 16 * TILES // 2)
            wait(pool, x_stored, 32)
            nc.gpsimd.iota(iota_e[:], [[1, E]], base=0, channel_multiplier=0).then_inc(iotas, 1)
            nc.gpsimd.iota(iota_s[:], [[1, 16]], base=0, channel_multiplier=0).then_inc(iotas, 1)
            nc.gpsimd.iota(tokid[:], [[P, TILES]], base=0, channel_multiplier=1).then_inc(iotas, 1)
            nc.gpsimd.iota(nobody[:], [[0, SC]], base=1 << 20, channel_multiplier=0).then_inc(nobody_ready, 1)
            nc.gpsimd.memset(tri[:], 1.0).then_inc(iotas, 1)
            pool.wait_ge(iotas, 4)
            nc.gpsimd.affine_select(out=tri[:], in_=tri[:], compare_op=ALU.is_gt, fill=0.0, base=0,
                                    pattern=[[1, P]], channel_multiplier=-1).then_inc(iotas, 1)
            nc.gpsimd.memset(zg[:], 0.0).then_inc(rows_zero, 1)
            nc.gpsimd.memset(xg[:], 0.0).then_inc(rows_zero, 1)
            pool.wait_ge(slots_ready, 1)
            pool.wait_ge(table_clear, 16)
            for t in range(TILES):
                pool.indirect_dma_start(slot_dram, bass.IndirectOffsetOnAxis(sloti[:, 3, t:t + 1], 0),
                                        tokid[:, t:t + 1], None).then_inc(table_set, 16)
            pool.wait_ge(table_in, 16)
            pool.wait_ge(rows_zero, 2)

            def gather(i, s, index, ready, rows, source, arrived):
                par = s % 2
                pool.sem_inc(pool_passed, 1)
                nc.gpsimd.tensor_copy(index[:, 2 * par:2 * par + 2], table[:, bass.ds(i * 4 + 2 * s, 2)]).then_inc(ready, 1)
                wait(pool, ready, i * 2 + (s + 1))
                pool.sem_inc(pool_passed, 1)
                for h in range(2):
                    pool.indirect_dma_start(rows[:, par, h], None, source,
                                            bass.IndirectOffsetOnAxis(index[:, 2 * par + h:2 * par + h + 1], 0),
                                            bounds_check=last_row, oob_is_err=False).then_inc(arrived[par], 16)

            def gather_z(i, s):
                wait(pool, tr_mm, i * 8 + 4 * (s - 1))
                gather(i, s, zidx, zidx_ready, zg, z_dram, zg_in)

            def gather_x(i, s):
                wait(pool, out_done[s % 2], i * 32 + 32 * (s // 2))
                gather(i, s, xidx, xidx_ready, xg, x_dram, xg_in)

            def scatter(i, s):
                par = s % 2
                wait(pool, y_ready, i * 8 + 4 * (s + 1))
                pool.sem_inc(pool_passed, 1)
                for h in range(2):
                    pool.indirect_dma_start(out, bass.IndirectOffsetOnAxis(xidx[:, 2 * par + h:2 * par + h + 1], 0),
                                            xg[:, par, h], None,
                                            bounds_check=last_row, oob_is_err=False).then_inc(out_done[par], 16)

            def tile(i, s):
                left = NS if not isinstance(i, int) else NS - 2 * i - s
                if left > 3:
                    gather_z(i, s + 3)
                scatter(i, s)
                if left > 2:
                    gather_x(i, s + 2)

            gather_z(0, 0)
            gather_z(0, 1)
            gather_x(0, 0)
            gather_x(0, 1)
            gather_z(0, 2)
            for i in rounds(pool, NS // 2, last=True):
                tile(i, 0)
                tile(i, 1)
            tile(NS // 2, 0)
            pool.wait_ge(out_done[0], 32 * (NS // 2 + 1))
            pool.wait_ge(out_done[1], 32 * (NS // 2))
            pool.wait_ge(w_stored[0], 16 * JOBS // 2)
            pool.wait_ge(w_stored[1], 16 * JOBS // 2)

        @block.scalar
        def _(act):
            act.wait_ge(mlp_mm, 1)
            nc.scalar.activation(hid1[:], bank[4][:, 0:B], ACT.Gelu, bias=b0s[:, 0:1]).then_inc(mlp_act, 1)
            act.wait_ge(mlp_mm, 2)
            nc.scalar.activation(hid2[:], bank[5][:, 0:B], ACT.Gelu, bias=b1s[:, 0:1]).then_inc(mlp_act, 1)
            act.wait_ge(mlp_dve, 2)
            nc.scalar.activation(satt[:, 0:E], bank[6][0:B, 0:E], ACT.Exp, bias=satt[:, 2 * E:2 * E + 1],
                                 accum_out=satt[:, 2 * E + 1:2 * E + 2]).then_inc(mlp_act, 1)
            act.wait_ge(bds_stored, 16)
            for blk in range(STEPS):
                def look(out, i, n, m):
                    sign, scale, bend = TERMS[m]
                    return nc.scalar.activation(out, codes[:, n % 2], ACT.Relu, scale=scale, bias=-scale * bend)

                def head(i, n, terms):
                    for m in terms:
                        if m == 0:
                            act.wait_ge(codes_in[n % 2], i * 64 + 16 * (n // 2 + 1))
                            wait_place(act, i, n, 0)
                        else:
                            wait(act, head_added, i * 16 + (2 * n + m - 1))
                        look(whole(n) if m == 0 else hterm[:], i, n, m).then_inc(head_terms, 1)

                def chain(i, n, terms):
                    for m in terms:
                        wait(act, term_added, i * (8 * NCH) + (NCH * n + m - 1))
                        look(term[:, (NCH * n + m) % 2], i, n, m + NHEAD).then_inc(term_ready, 1)

                def high(i, n):
                    if blk == 0:
                        act.wait_ge(w_ready, i * 8 + (n + 1))
                        act.dma_start(w_dram[bass.ds(i * 8 + n, 1)].rearrange("a p n -> p (a n)"),
                                      whole(n)).then_inc(w_stored[n % 2], 16)
                    else:
                        act.wait_ge(w_in[n % 8], i * 16 + 16 * (n // 8 + 1))
                    if isinstance(i, int) and i == 0 and n == 7:
                        act.wait_ge(acc_bias, PAIRS * (blk + 1))
                    nc.scalar.activation(high_part(n), whole(n), ACT.Copy).then_inc(wh_ready, 1)

                def relu(i, w):
                    act.wait_ge(up_mm, i * 4 + (NU * blk + w + 1))
                    act.sem_inc(act_passed, 1)
                    for s in range(2):
                        nc.scalar.activation(bank[s], bank[s], ACT.Relu,
                                             bias=bup[:, bass.ds(i * 4 + (2 * (w // 2) + s), 1)]).then_inc(relu_done, 1)
                    wait(act, dn_mm, i * 16 + 4 * (NU * blk + w - 1))
                    act.wait_ge(relu_done, i * 8 + 2 * (NU * blk + w + 1))
                    h = 2 * (w % 2)
                    nc.scalar.activation(hh[:, h:h + 2], pair[0][:].rearrange("p (s t) -> p s t", s=2), ACT.Copy).then_inc(hh_ready, 1)

                def prepare(i, n, more=True, unit=None):
                    first = isinstance(i, int) and i * 8 + n == 0
                    if blk == 0:
                        chain(i, n, range(0, 3))
                        if not first:
                            high(i, n - 1)
                        if more:
                            head(i, n + 1, (0, 1))
                        chain(i, n, range(3, 4))
                        if unit:
                            relu(*unit)
                        if more:
                            head(i, n + 1, (2,))
                        chain(i, n, range(4, NCH))
                    else:
                        if not first:
                            high(i, n - 1)
                        if unit:
                            relu(*unit)

                def conv_high(i, batches):
                    for k in batches:
                        act.wait_ge(x32_ready, i * 4 + (BB * blk + k + 1))
                        act.sem_inc(act_passed, 1)
                        nc.scalar.activation(x1h[:, :, bass.ds(i * 4 * CH + k * CH, CH)], x32[:, k % 2], ACT.Copy).then_inc(x1h_ready, 1)

                def z_bias(i, p):
                    done = PAIRS * (blk - 1) + p
                    act.wait_ge(z_mm, i * 2 + (done + 1))
                    wait(act, z_stored[p % 2], i * 16 + 16 * (done // 2))
                    wait(act, z_tr, i * 2 + (done - 1))
                    nc.scalar.activation(z32[:, p % 2], pair[0][:], ACT.Identity,
                                         bias=aggb[:, bass.ds(i * 2 + done, 1)]).then_inc(z_ready, 1)

                if blk == 0:
                    act.wait_ge(ffn_const, 48)
                    act.wait_ge(aggb_ready, 2)
                    head(0, 0, (0, 1, 2))
                    for i in range(4):
                        conv_high(i, range(4))
                        prepare(0, i)
                else:
                    z_bias(0, 0)
                    for i in rounds(act, PAIRS // 2, last=True):
                        if blk < BLKS:
                            conv_high(i, (0, 1))
                        z_bias(i, 1)
                        if blk < BLKS:
                            conv_high(i, (2, 3))
                        if not isinstance(i, int) or i < PAIRS // 2 - 1:
                            z_bias(i, 2)
                if blk == BLKS:
                    break
                for n in range(0 if blk else 4, AHEAD):
                    prepare(0, n, unit=(0, 0) if n == 4 else None)
                for i in rounds(act, ROUNDS, last=True):
                    for k in range(4):
                        jobs = stage_jobs(i, k)
                        if jobs:
                            prepare(*jobs[0], unit=(i, k + 1))
                            prepare(*jobs[1], more=not isinstance(i, int) or i * 8 + jobs[1][1] < JOBS - 1)
                        else:
                            high(0, JOBS - 1)
                            relu(i, k + 1)
                relu(ROUNDS, 1)

            def chunk_high(i, par, kt):
                act.wait_ge(wraw_in[kt], i * 32 + (16 * par + 16))
                wait(act, chunk_mm, i * 16 + (8 * par + kt - 3))
                nc.scalar.activation(whr[:, kt % 4], wraw[:, kt], ACT.Copy).then_inc(whr_ready, 1)

            def z_high(i, par):
                for b in range(4):
                    act.wait_ge(tr_mm, i * 8 + (4 * par + b + 1))
                    wait(act, chunk_mm, i * 16 + (8 * par - 8))
                    nc.scalar.activation(zth[:, par, 2 * b:2 * b + 2], bank[4 * par + b][:].rearrange("p (k s) -> p k s", k=2),
                                         ACT.Copy).then_inc(zth_ready, 1)

            def expert(i, par, nxt):
                for kt in range(KT):
                    chunk_high(i, par, kt)
                    if kt == 5 and nxt:
                        z_high(*nxt)

            wait(act, logit_ready, TILES)
            for k in range(2):
                wait(act, z_stored[k], 16 * TILES // 2)
            z_high(0, 0)
            for i in rounds(act, NS // 2):
                expert(i, 0, (i, 1))
                expert(i, 1, (i + 1, 0))
            expert(NS // 2, 0, None)

        @block.vector
        def _(dve):
            dve.wait_ge(mlp_mm, 3)
            nc.vector.reduce_max(satt[:, 2 * E + 2:2 * E + 3], bank[6][0:B, 0:E], AX.X).then_inc(mlp_dve, 1)
            dve.wait_ge(mlp_dve, 1)
            nc.vector.tensor_scalar(satt[:, 2 * E:2 * E + 1], satt[:, 2 * E + 2:2 * E + 3], -1.0, None,
                                    ALU.mult).then_inc(mlp_dve, 1)
            dve.wait_ge(mlp_act, 3)
            nc.vector.reciprocal(satt[:, 2 * E + 3:2 * E + 4], satt[:, 2 * E + 1:2 * E + 2]).then_inc(mlp_dve, 1)
            dve.wait_ge(mlp_dve, 3)
            nc.vector.tensor_scalar(satt[:, E:2 * E], satt[:, 0:E], satt[:, 2 * E + 3:2 * E + 4], None,
                                    ALU.mult).then_inc(mlp_dve, 1)
            dve.wait_ge(mlp_mm, 4)
            nc.vector.tensor_copy(att_t[:], bank[7][0:E, 0:B]).then_inc(att_ready, 1)
            dve.wait_ge(agg_mm, 1)
            dve.wait_ge(bds_zero, 1)
            for c in range(2):
                rows = slice(64 * c, 64 * c + 64)
                for h in range(4):
                    src = bank[h][rows, :].rearrange("p (o q c) -> p q o c", q=TILES, c=2)[:, :, :, c]
                    nc.vector.tensor_copy(bds[rows, :, 64 * c + 16 * h:64 * c + 16 * h + 16], src).then_inc(agg_ready, 1)
                nc.vector.tensor_copy(aggb[rows, :], bank[6][rows, 0:B].rearrange("p (q c) -> p q c", c=2)[:, :, c]).then_inc(aggb_ready, 1)
            for blk in range(STEPS):
                def chain(i, n, terms):
                    if not blk:
                        for m in terms:
                            dve.wait_ge(term_ready, i * (8 * NCH) + (NCH * n + m + 1))
                            if m == 0:
                                dve.wait_ge(head_added, i * 16 + 2 * (n + 1))
                            else:
                                dve.wait_ge(term_added, i * (8 * NCH) + (NCH * n + m))
                            op = ALU.add if CHAIN[m][0] > 0 else ALU.subtract
                            nc.vector.tensor_tensor(whole(n), whole(n), term[:, (NCH * n + m) % 2], op).then_inc(term_added, 1)

                def add_lora(i, n):
                    if not blk:
                        dve.wait_ge(ab_mm, i * 8 + (n + 1))
                        dve.wait_ge(scaled, i * 8 + (n + 1))
                        nc.vector.tensor_tensor(whole(n), whole(n), pair[1][:], ALU.add).then_inc(w_ready, 1)

                def low(i, n):
                    if blk:
                        dve.wait_ge(wh_ready, i * 8 + (JOBS * blk + n + 1))
                        nc.vector.tensor_tensor(low_part(n), whole(n), high_part(n), ALU.subtract).then_inc(wl_ready, 1)

                def fill(n):
                    chain(0, n, range(2))
                    if n:
                        add_lora(0, n - 1)
                        low(0, n - 1)
                    chain(0, n, range(2, NCH))
                    if n == 4:
                        hidden_low(0, 0)

                def hidden_low(i, w):
                    dve.wait_ge(hh_ready, i * 4 + (NU * blk + w + 1))
                    h = 2 * (w % 2)
                    nc.vector.tensor_tensor(hl[:, h:h + 2], pair[0][:].rearrange("p (s t) -> p s t", s=2), hh[:, h:h + 2],
                                            ALU.subtract).then_inc(hl_ready, 1)

                def add_down(i, u, j):
                    dve.wait_ge(dn_mm, i * 16 + (4 * (NU * blk + u) + j + 1))
                    if isinstance(i, int) and i == 0 and u < 2:
                        dve.wait_ge(acc_bias, PAIRS * blk + 4 * u + j + 1)
                    else:
                        wait(dve, acc_added, i * 16 + (4 * (NU * blk + u - 2) + j + 1))
                    a = acc[:, 4 * (u % 2) + j]
                    nc.vector.tensor_tensor(a, a, pair[2 + j % 2][:], ALU.add).then_inc(acc_added, 1)

                def conv_low(i, k):
                    dve.wait_ge(x1h_ready, i * 4 + (BB * blk + k + 1))
                    o = x1l[:, :, bass.ds(i * 4 * CH + k * CH, CH)]
                    nc.vector.tensor_tensor(o, x32[:, k % 2], x1h[:, :, bass.ds(i * 4 * CH + k * CH, CH)],
                                            ALU.subtract).then_inc(x1l_ready, 1)

                def conv_sum(i, k):
                    dve.wait_ge(conv_mm, i * 4 + (BB * blk + k + 1))
                    wait(dve, x1l_ready, i * 4 + (BB * blk + k - 1))
                    cx = ctxb[:, bass.ds(i * 4 * CH + k * CH, CH)].rearrange("p (j g o) -> p j g o", j=1, g=GROUPS)
                    nc.vector.tensor_tensor(x32[:, k % 2].rearrange("p j (g o) -> p j g o", g=GROUPS),
                                            bank[4 + k % 2].rearrange("p (g j o) -> p j g o", g=GROUPS, j=J),
                                            cx.broadcast_to([P, J, GROUPS, GC]), ALU.add).then_inc(x32_ready, 1)

                def z_copied(i, k):
                    done = PAIRS * (blk - 1) + k
                    dve.wait_ge(z_tr, i * 2 + (done + 1))
                    wait(dve, gate_mm, i * 2 + done)
                    nc.vector.tensor_copy(zt[:], pair[1][:]).then_inc(zt_ready, 1)

                def logit(i, k):
                    done = PAIRS * (blk - 1) + k
                    dve.wait_ge(gate_mm, i * 2 + (done + 1))
                    nc.vector.tensor_copy(logits[:, bass.ds(i * 2 + done, 1)],
                                          bank[6 + k][:, 0:E].rearrange("p (a e) -> p a e", a=1)).then_inc(logit_ready, 1)

                if blk < BLKS:
                    dve.wait_ge(conv_const, 64 * (blk + 1))
                    cb = ct[:, BB * blk:BB * (blk + 1)].rearrange("p (b o) -> p b o", o=1).broadcast_to([P, BB, CH])
                    cw = cwt[:].rearrange("p (b o) -> p b o", b=1).broadcast_to([P, BB, CH])
                    nc.vector.tensor_tensor(cprod[:], cb, cw, ALU.mult).then_inc(cprod_ready, 1)
                    dve.wait_ge(ctx_mm, blk + 1)
                    for h in range(2):
                        nc.vector.tensor_copy(ctxb[:, h * 512:(h + 1) * 512], bank[h]).then_inc(ctxb_ready, 1)
                    dve.wait_ge(ctxb_ready, 2 * (blk + 1))

                def step(i):
                    for k in range(2):
                        if blk < BLKS:
                            conv_sum(i, 2 * k)
                            conv_sum(i, 2 * k + 1)
                            conv_low(i, 2 * k)
                        if blk:
                            z_copied(i, k)
                        if blk < BLKS:
                            conv_low(i, 2 * k + 1)
                        if blk:
                            logit(i, k)

                if blk == 0:
                    for i in range(4):
                        step(i)
                        fill(i)
                else:
                    for i in rounds(dve, PAIRS // 2):
                        step(i)
                if blk == BLKS:
                    break
                for n in range(0 if blk else 4, AHEAD):
                    fill(n)
                for i in rounds(dve, ROUNDS, last=True):
                    for k in range(4):
                        jobs = stage_jobs(i, k)
                        if jobs:
                            a, b = jobs
                            chain(*a, range(0, 2))
                            add_lora(i, a[1] - 1)
                            low(i, a[1] - 1)
                            chain(*a, range(2, 4))
                            hidden_low(i, k + 1)
                            add_down(i, k, 0)
                            low(*a)
                            chain(*a, range(4, NCH))
                            chain(*b, range(0, 1))
                            add_down(i, k, 1)
                            chain(*b, range(1, 2))
                            add_lora(*a)
                            chain(*b, range(2, 3))
                            add_down(i, k, 2)
                            chain(*b, range(3, 4))
                            add_down(i, k, 3)
                            chain(*b, range(4, NCH))
                        else:
                            add_lora(0, JOBS - 1)
                            low(0, JOBS - 1)
                            hidden_low(i, k + 1)
                            for j in range(4):
                                add_down(i, k, j)
                for j in range(4):
                    add_down(ROUNDS, 0, j)
                    if j == 0:
                        hidden_low(ROUNDS, 1)
                for j in range(4):
                    add_down(ROUNDS, 1, j)

            step = [0]

            def link(ins):
                step[0] += 1
                ins.then_inc(route_dve, 1)
                dve.wait_ge(route_dve, step[0])

            dve.wait_ge(logit_ready, TILES)
            for k in range(2):
                dve.wait_ge(z_stored[k], 16 * TILES // 2)
            dve.wait_ge(x_stored, 32)
            dve.wait_ge(iotas, 5)
            for t in range(TILES):
                ins = nc.vector.max(top[:, t], logits[:, t])
            link(ins)
            for t in range(TILES):
                ins = nc.vector.max_index(topi[:, t], top[:, t], logits[:, t])
            link(ins)
            nc.vector.tensor_copy(iota_sf[:], iota_s[:])
            nc.vector.tensor_copy(iota_ef[:], iota_e[:])
            link(nc.vector.tensor_copy(eid[:], topi[:, :, 0]))
            link(nc.vector.tensor_tensor(oh[:], eid[:].rearrange("p (t o) -> p t o", o=1).broadcast_to([P, TILES, E]),
                                         iota_ef[:].rearrange("p (o e) -> p o e", o=1).broadcast_to([P, TILES, E]), ALU.is_equal))
            link(nc.vector.memset(run[:, 0], 0.0))
            dve.wait_ge(route_mm, 1)
            total = bank[1][:, 0:P].rearrange("p (t e) -> p t e", e=E)
            for t in range(TILES):
                link(nc.vector.tensor_tensor(run[:, t + 1], run[:, t], total[:, t], ALU.add))
            link(nc.vector.tensor_scalar(cnt[:], run[:, TILES], float(ST - 1), None, ALU.add))
            link(nc.vector.tensor_single_scalar(cnt2[:], cnt[:], ST.bit_length() - 1, ALU.arith_shift_right))
            link(nc.vector.tensor_copy(ntl[:], cnt2[:]))
            link(nc.vector.memset(end[:, 0:1], 0.0))
            for e in range(E):
                link(nc.vector.tensor_tensor(end[:, e + 1:e + 2], end[:, e:e + 1], ntl[:, e:e + 1], ALU.add))
            link(nc.vector.tensor_tensor(place[:], bank[0][:, 0:P].rearrange("p (t e) -> p t e", e=E), run[:, 0:TILES], ALU.add))
            link(nc.vector.scalar_tensor_tensor(out=place[:], in0=end[:, 0:E].rearrange("p (o e) -> p o e", o=1).broadcast_to([P, TILES, E]),
                                                scalar=float(ST), in1=place[:], op0=ALU.mult, op1=ALU.add))
            link(nc.vector.tensor_tensor(place[:], place[:], oh[:], ALU.mult))
            link(nc.vector.reduce_sum(slotf[:], place[:], AX.X))
            link(nc.vector.tensor_copy(sloti[:, 0], slotf[:]))
            nc.vector.tensor_single_scalar(sloti[:, 1], sloti[:, 0], P - 1, ALU.bitwise_and)
            link(nc.vector.tensor_single_scalar(sloti[:, 2], sloti[:, 0], P.bit_length() - 1, ALU.arith_shift_right))
            link(nc.vector.tensor_copy(slotp[:], sloti[:, 1:3]))
            nc.vector.scalar_tensor_tensor(out=sloti[:, 3], in0=slotp[:, 0], scalar=float(SC), in1=slotp[:, 1], op0=ALU.mult,
                                           op1=ALU.add).then_inc(slots_ready, 1)
            link(nc.vector.tensor_tensor(past[:], end[:, 1:E + 1].rearrange("p (o e) -> p o e", o=1).broadcast_to([P, 16, E]),
                                         iota_sf[:].rearrange("p (s o) -> p s o", o=1).broadcast_to([P, 16, E]), ALU.is_le))
            link(nc.vector.reduce_sum(etf[:], past[:], AX.X))
            nc.vector.tensor_scalar(eti[:], etf[:], float(E - 1), None, ALU.min).then_inc(tiles_ready, 1)

            def chunk_low(i, par, kt):
                dve.wait_ge(whr_ready, i * 16 + (8 * par + kt + 1))
                nc.vector.tensor_tensor(wlr[:, kt % 4], wraw[:, kt], whr[:, kt % 4], ALU.subtract).then_inc(wlr_ready, 1)

            def z_low(i, par):
                for b in range(4):
                    dve.wait_ge(zth_ready, i * 8 + (4 * par + b + 1))
                    nc.vector.tensor_tensor(ztl[:, par, 2 * b:2 * b + 2], bank[4 * par + b][:].rearrange("p (k s) -> p k s", k=2),
                                            zth[:, par, 2 * b:2 * b + 2], ALU.subtract).then_inc(ztl_ready, 1)

            def add_bias(i, par):
                dve.wait_ge(eb_in[par], i * 16 + 16)
                dve.wait_ge(xg_in[par], i * 32 + 32)
                a = xg[:, par]
                nc.vector.tensor_tensor(a, a, ebs[:, par:par + 1].broadcast_to([P, 2, L]), ALU.add).then_inc(xb_ready, 1)

            def add_rows(i, par):
                wait(dve, chunk_mm, i * 16 + (8 * par + 8))
                dve.wait_ge(xb_ready, i * 2 + (par + 1))
                for b in range(4):
                    a = xg[:, par, b // 2, (b % 2) * 512:(b % 2 + 1) * 512]
                    nc.vector.tensor_tensor(a, a, bank[4 * par + b], ALU.add).then_inc(y_ready, 1)

            def expert(i, par, nxt, last):
                for kt in range(KT):
                    chunk_low(i, par, kt)
                    if kt == 0 and last:
                        add_rows(*last)
                    if kt == 3:
                        add_bias(i, par)
                    if kt == 5 and nxt:
                        z_low(*nxt)

            z_low(0, 0)
            for i in rounds(dve, NS // 2):
                expert(i, 0, (i, 1), (i - 1, 1) if not isinstance(i, int) else None)
                expert(i, 1, (i + 1, 0), (i, 0))
            expert(NS // 2, 0, None, (NS // 2 - 1, 1))
            add_rows(NS // 2, 0)

        @block.tensor
        def _(pe):
            mm = nc.tensor.matmul

            def three(ps, ah, al, bh, bl, first, last):
                mm(ps, ah, bh, start=first, stop=False)
                mm(ps, ah, bl, start=False, stop=False)
                return mm(ps, al, bh, start=False, stop=last)

            pe.wait_ge(ident_ready, 2)
            pe.wait_ge(ones_ready, 1)
            pe.wait_ge(mlp_const, 16 * MLP_CONSTS)
            mm(bank[4][:, 0:B], w0s[:], ct2[:], start=True, stop=True).then_inc(mlp_mm, 1)
            pe.wait_ge(mlp_act, 1)
            mm(bank[5][:, 0:B], w1s[:], hid1[:], start=True, stop=True).then_inc(mlp_mm, 1)
            pe.wait_ge(mlp_act, 2)
            mm(bank[6][0:B, 0:E], hid2[:], w2s[:], start=True, stop=False)
            mm(bank[6][0:B, 0:E], ones[0:1, 0:B], b2s[:], start=False, stop=True).then_inc(mlp_mm, 1)
            pe.wait_ge(mlp_dve, 4)
            nc.tensor.transpose(bank[7][0:E, 0:B], satt[:, E:2 * E], ident[0:B, 0:B]).then_inc(mlp_mm, 1)
            pe.wait_ge(att_ready, 1)
            for o in range(CH):
                mm(bank[o // 16][:, (o % 16) * B:(o % 16 + 1) * B], kerns[:, o], att_t[:], start=True, stop=True)
            mm(bank[6][:, 0:B], kernb[:], att_t[:], start=True, stop=True).then_inc(agg_mm, 1)

            for blk in range(STEPS):
                def lora_product(i, n):
                    if blk:
                        return
                    s = n % 2
                    if n % 4 < 2:
                        pe.wait_ge(lora_in[s], i * 64 + 32 * (n // 4 + 1))
                    wait(pe, w_ready, i * 8 + n)
                    for h in range(2):
                        if n % 4 < 2:
                            for q in range(4):
                                ins = mm(bank[2 + h][:, q * P:(q + 1) * P], lora[0:R, (4 * h + q) * P:(4 * h + q + 1) * P],
                                         lora_t[0:R, s], start=True, stop=True)
                        else:
                            ins = mm(bank[2 + h], lora_t[32:32 + R, s], lora[32:32 + R, h * 512:(h + 1) * 512],
                                     start=True, stop=True)
                    ins.then_inc(ab_mm, 1)

                def up(i, w, between=None):
                    half, par = w % 2, (w // 2) % 2
                    pe.wait_ge(wl_ready, i * 8 + (JOBS * blk + 4 * (w // 2) + 2))
                    wait(pe, hl_ready, i * 4 + (NU * blk + w))
                    t0 = half * HALF
                    for s in range(2):
                        for kt in range(KT):
                            c = slice(kt * P, (kt + 1) * P)
                            ins = three(bank[s], wuh[:, 2 * par + s, c], wul[:, 2 * par + s, c], x1h[:, kt, t0:t0 + HALF],
                                        x1l[:, kt, t0:t0 + HALF], kt == 0, kt == KT - 1)
                        if s == 0 and between:
                            lora_product(*between)
                    ins.then_inc(up_mm, 1)

                def down(i, u, between=None):
                    par, hp = (u // 2) % 2, u % 2
                    pe.wait_ge(wl_ready, i * 8 + (JOBS * blk + 4 * (u // 2) + 4))
                    pe.wait_ge(hl_ready, i * 4 + (NU * blk + u + 1))
                    for j in range(4):
                        wait(pe, acc_added, i * 16 + (4 * (NU * blk + u) + j - 1))
                        c = slice(j * P, (j + 1) * P)
                        for dh in range(2):
                            d = slice(dh * 512, (dh + 1) * 512)
                            for s in range(2):
                                ins = three(bank[4 + 2 * (j % 2) + dh], hh[:, 2 * hp + s, c], hl[:, 2 * hp + s, c],
                                            wdh[:, 2 * par + s, d], wdl[:, 2 * par + s, d], s == 0, s == 1)
                        ins.then_inc(dn_mm, 1)
                        if j == 1 and between:
                            lora_product(*between)

                def conv(i, k):
                    if k % 2 == 0:
                        pe.wait_ge(xcv_in[k // 2], i * 16 + (16 * PAIRS // 2 * blk + 16))
                    wait(pe, x32_ready, i * 4 + (BB * blk + k - 1))
                    for g in range(GROUPS):
                        for d in range(2):
                            ins = mm(bank[4 + k % 2][:, g * P:(g + 1) * P], xcv[:, k // 2, k % 2, g, d:d + P], tz[:, d, g],
                                     start=d == 0, stop=d == 1)
                    ins.then_inc(conv_mm, 1)

                def z_product(i, p):
                    done = PAIRS * (blk - 1) + p
                    pe.wait_ge(bdg_in[p % 2], i * 16 + 16 * (done // 2 + 1))
                    wait(pe, z_ready, i * 2 + done)
                    for h in range(2):
                        rows = acc[:, bass.ds(i * 2 + p, 1), h * 512:(h + 1) * 512].rearrange("p a l -> p (a l)")
                        ins = mm(bank[h], bdg[:, p % 2], rows, start=True, stop=True)
                    ins.then_inc(z_mm, 1)

                def z_transposed(i, p):
                    done = PAIRS * (blk - 1) + p
                    pe.wait_ge(z_ready, i * 2 + (done + 1))
                    wait(pe, zt_ready, i * 2 + done)
                    for kt in range(KT):
                        ins = nc.tensor.transpose(pair[1][:, kt * P:(kt + 1) * P], z32[:, p % 2, kt * P:(kt + 1) * P], ident[:])
                    ins.then_inc(z_tr, 1)

                def gate(i, p):
                    done = PAIRS * (blk - 1) + p
                    pe.wait_ge(zt_ready, i * 2 + (done + 1))
                    wait(pe, logit_ready, i * 2 + (done - 1))
                    mm(bank[6 + p][:, 0:E], ones[0:1, :], gbs[:], start=True, stop=False)
                    for kt in range(KT):
                        ins = mm(bank[6 + p][:, 0:E], zt[:, kt * P:(kt + 1) * P], gts[:, kt], start=False, stop=kt == KT - 1)
                    ins.then_inc(gate_mm, 1)

                wait(pe, acc_added, 4 * NU * blk)
                wait(pe, hl_ready, NU * blk)
                wait(pe, w_ready, JOBS if blk else 0)
                if blk == 0:
                    pe.wait_ge(agg_ready, 8)
                    pe.wait_ge(aggb_ready, 2)
                if blk < BLKS:
                    pe.wait_ge(cprod_ready, blk + 1)
                    for h in range(2):
                        mm(bank[h], ones[:], cprod[:, h * 8:(h + 1) * 8], start=True, stop=False)
                        ins = mm(bank[h], ones[0:1, :], cbias[:].rearrange("p (b o) -> p b o", b=1).broadcast_to([1, 8, CH]),
                                 start=False, stop=True)
                    ins.then_inc(ctx_mm, 1)
                if blk == 0:
                    pe.wait_ge(ffn_const, 48)
                    for i in range(4):
                        for k in range(4):
                            conv(i, k)
                        if i < 3:
                            lora_product(0, i)
                else:
                    if blk < BLKS:
                        pe.wait_ge(ctxb_ready, 2 * (blk + 1))
                    z_product(0, 0)
                    for i in rounds(pe, PAIRS // 2, last=True):
                        for k in range(2):
                            if blk < BLKS:
                                conv(i, 2 * k)
                            z_transposed(i, k)
                            if k == 0 or not isinstance(i, int) or i < PAIRS // 2 - 1:
                                z_product(i, k + 1)
                            if blk < BLKS:
                                conv(i, 2 * k + 1)
                            gate(i, k)
                if blk == BLKS:
                    break
                pe.wait_ge(x1l_ready, BB * (blk + 1))
                if blk:
                    for n in range(3):
                        lora_product(0, n)
                up(0, 0, (0, 3))
                lora_product(0, 4)
                for i in rounds(pe, ROUNDS, last=True):
                    for k in range(4):
                        jobs = stage_jobs(i, k)
                        up(i, k + 1, (i, 5 + 2 * k))
                        down(i, k, jobs[0] if jobs else None)
                up(ROUNDS, 1)
                down(ROUNDS, 0)
                down(ROUNDS, 1)

            pe.wait_ge(route_dve, ONEHOT)
            pe.wait_ge(iotas, 5)
            mm(bank[0][:, 0:P], tri[:], oh[:].rearrange("p t e -> p (t e)"), start=True, stop=True)
            mm(bank[1][:, 0:P], ones[:], oh[:].rearrange("p t e -> p (t e)"), start=True, stop=True).then_inc(route_mm, 1)
            pe.wait_ge(slots_ready, 1)

            def rows_transposed(i, par):
                pe.wait_ge(zg_in[par], i * 32 + 32)
                wait(pe, y_ready, i * 8 + (4 * par - 4))
                for b in range(4):
                    for q in range(4):
                        kt, h = 2 * b + q // 2, q % 2
                        ins = nc.tensor.transpose(bank[4 * par + b][:, q * P:(q + 1) * P], zg[:, par, h, kt * P:(kt + 1) * P], ident[:])
                    ins.then_inc(tr_mm, 1)

            def chunk(i, par, kt):
                pe.wait_ge(wlr_ready, i * 16 + (8 * par + kt + 1))
                if kt == 0:
                    pe.wait_ge(ztl_ready, i * 8 + (4 * par + 4))
                for b in range(4):
                    s, d = slice((b // 2) * P, (b // 2 + 1) * P), slice((b % 2) * 512, (b % 2 + 1) * 512)
                    ins = three(bank[4 * par + b][:], zth[:, par, kt, s], ztl[:, par, kt, s], whr[:, kt % 4, d], wlr[:, kt % 4, d],
                                kt == 0, kt == KT - 1)
                ins.then_inc(chunk_mm, 1)

            def expert(i, par, nxt):
                for kt in range(KT):
                    chunk(i, par, kt)
                    if kt == 3 and nxt:
                        rows_transposed(*nxt)

            rows_transposed(0, 0)
            for i in rounds(pe, NS // 2):
                expert(i, 0, (i, 1))
                expert(i, 1, (i + 1, 0))
            expert(NS // 2, 0, None)


def layouts(x, cond_128, fside_S_0, L0_cond_weight, L0_cond_c_weight, L0_ffn_w_up_codes, L0_ffn_w_up_absmax,
            L0_ffn_b_up, L0_ffn_w_up_lora_a, L0_ffn_w_up_lora_b, L0_ffn_w_down_codes, L0_ffn_w_down_absmax, L0_ffn_b_down,
            L0_ffn_w_down_lora_a, L0_ffn_w_down_lora_b, L1_cond_W0, L1_cond_b0, L1_cond_W1, L1_cond_b1, L1_cond_W2,
            L1_cond_b2, L1_cond_weight, L1_cond_bias_k, L1_ffn_gate_w, L1_ffn_gate_b, L1_ffn_expert_w, L1_ffn_expert_b):
    def padded(a, axis, size):
        room = [(0, 0)] * a.ndim
        room[axis] = (0, size - a.shape[axis])
        return np.pad(a, room)

    half = TAPS // 2
    xp = np.pad(x, ((0, 0), (0, 0), (half, J * MB - L - half)))
    x_conv = xp.reshape(B, GROUPS, GC, MB, J).transpose(2, 4, 0, 1, 3).reshape(P, B, GROUPS, MB)
    w = L0_cond_weight.reshape(GROUPS, GC, GC, TAPS)
    toep = np.zeros((GC, J, 2, GROUPS, J, GC), w.dtype)
    for d in range(2):
        for jp in range(J):
            for j in range(J):
                tap = J * d + jp - j
                if 0 <= tap < TAPS:
                    toep[:, jp, d, :, j, :] = w[:, :, :, tap].transpose(2, 0, 1)
    cu = padded(L0_ffn_w_up_codes.reshape(HID, P, J), 0, NT * P).reshape(NT, P, P, J).transpose(0, 2, 3, 1)
    cd = padded(L0_ffn_w_down_codes.reshape(L, HID).T, 0, NT * P).reshape(NT, P, L)
    au = padded(L0_ffn_w_up_absmax.reshape(HID, 16), 0, NT * P).reshape(NT, P, 16).transpose(0, 2, 1)
    ad = padded(L0_ffn_w_down_absmax.reshape(L, HID // 64).T, 0, 2 * NT).reshape(NT, 2, L)
    kern = L1_cond_weight[..., 0]
    return dict(
        x_nat=x.reshape(N, L), x_conv=x_conv, toep=toep.reshape(P, 2, GROUPS, P), cond_t=cond_128.T,
        ctx_w_t=L0_cond_c_weight.T, chan_bias=fside_S_0.reshape(1, CH), codes_up=cu.reshape(NT, P, L), codes_dn=cd,
        am_up=au, am_dn=ad, bias_up=padded(L0_ffn_b_up, 0, NT * P).reshape(NT, P).T, bias_dn=L0_ffn_b_down.reshape(1, L),
        lora_up_at=L0_ffn_w_up_lora_a.reshape(P, J, R).transpose(2, 1, 0).reshape(R, L),
        lora_up_b=padded(L0_ffn_w_up_lora_b, 1, NT * P).reshape(R, NT, P).transpose(1, 0, 2),
        lora_dn_at=padded(L0_ffn_w_down_lora_a, 0, NT * P).reshape(NT, P, R).transpose(0, 2, 1),
        lora_dn_b=L0_ffn_w_down_lora_b, w0=L1_cond_W0, b0=L1_cond_b0.reshape(P, 1), w1=L1_cond_W1,
        b1=L1_cond_b1.reshape(P, 1), w2=L1_cond_W2, b2=L1_cond_b2.reshape(1, E),
        kern=np.concatenate([kern, kern], 2), kern_b=np.concatenate([L1_cond_bias_k] * 2, 1),
        gate_t=L1_ffn_gate_w.T.reshape(KT, P, E).transpose(1, 0, 2), gate_b=L1_ffn_gate_b.reshape(1, E),
        exp_w=L1_ffn_expert_w.transpose(0, 2, 1).reshape(E, KT, P, L).transpose(0, 2, 1, 3), exp_b=L1_ffn_expert_b)


def kernel(**inputs):
    import concourse.bacc as bacc
    from concourse.bass_utils import run_bass_kernel_spmd

    arrays = {name: np.ascontiguousarray(a) for name, a in layouts(**{k: np.asarray(a) for k, a in inputs.items()}).items()}
    nc = bacc.Bacc("TRN2", target_bir_lowering=False, num_devices=1)
    args = {name: nc.dram_tensor(name, a.shape, mybir.dt.from_np(a.dtype), kind="ExternalInput").ap()
            for name, a in arrays.items()}
    out = nc.dram_tensor("out", (N, L), F32, kind="ExternalOutput").ap()
    program(nc, out=out, **args)
    result = run_bass_kernel_spmd(nc, [arrays], core_ids=[0])
    return result.results[0]["out"].reshape(B, CH, L)
```
